# Optimizing a Trainium2 kernel written in Bass

```python
import numpy as np
import jax
import jax.numpy as jnp

def _softmax(x, axis=-1):
    return jax.nn.softmax(x, axis=axis)

def _gelu(x):
    return jax.nn.gelu(x, approximate=True)

def _silu(x):
    return jax.nn.silu(x)

def _sigmoid(x):
    return jax.nn.sigmoid(x)

def _layernorm(x, axis=-1, eps=1e-05):
    m = jnp.mean(x, axis=axis, keepdims=True)
    v = jnp.var(x, axis=axis, keepdims=True)
    return (x - m) / jnp.sqrt(v + eps)

def _scatter_add(tgt, idx, src, axis=0):
    return tgt.at[idx].add(src)

def _segment_sum(src, seg, n):
    return jax.ops.segment_sum(src, seg, n)
kernel_name = 'mk_dlrm_tower_d1_rec_r8_1bdcd7'

def setup_inputs(seed: int=0):
    np.random.seed(seed)
    _w = jnp.asarray

    def _rec_inputs():
        import jax
        import jax.numpy as jnp
        _tk = jax.random.key(seed)
        dense_ctx = jax.random.normal(jax.random.fold_in(_tk, 190), (1024, 16), jnp.float32)
        ids = jnp.stack([jax.random.randint(jax.random.fold_in(_tk, 200 + f), (1024,), 0, v, jnp.int32) for f, v in enumerate([1250, 1250, 12500, 1000, 12500, 1000, 1000, 1250, 1000, 12500, 1250, 1250, 1000, 12500, 1000, 1000, 12500, 1250, 1000, 1250, 12500, 125000, 1000, 12500, 12500, 1250, 12500, 1250, 12500, 125000, 125000, 12500, 125000, 125000, 1250, 12500, 125000, 125000, 12500])], axis=1)
        tbl_0 = 0.05 * jax.random.normal(jax.random.fold_in(_tk, 500 + 0), (1250, 16), jnp.float32)
        tbl_1 = 0.05 * jax.random.normal(jax.random.fold_in(_tk, 500 + 1), (1250, 16), jnp.float32)
        tbl_2 = 0.05 * jax.random.normal(jax.random.fold_in(_tk, 500 + 2), (12500, 16), jnp.float32)
        tbl_3 = 0.05 * jax.random.normal(jax.random.fold_in(_tk, 500 + 3), (1000, 16), jnp.float32)
        tbl_4 = 0.05 * jax.random.normal(jax.random.fold_in(_tk, 500 + 4), (12500, 16), jnp.float32)
        tbl_5 = 0.05 * jax.random.normal(jax.random.fold_in(_tk, 500 + 5), (1000, 16), jnp.float32)
        tbl_6 = 0.05 * jax.random.normal(jax.random.fold_in(_tk, 500 + 6), (1000, 16), jnp.float32)
        tbl_7 = 0.05 * jax.random.normal(jax.random.fold_in(_tk, 500 + 7), (1250, 16), jnp.float32)
        tbl_8 = 0.05 * jax.random.normal(jax.random.fold_in(_tk, 500 + 8), (1000, 16), jnp.float32)
        tbl_9 = 0.05 * jax.random.normal(jax.random.fold_in(_tk, 500 + 9), (12500, 16), jnp.float32)
        tbl_10 = 0.05 * jax.random.normal(jax.random.fold_in(_tk, 500 + 10), (1250, 16), jnp.float32)
        tbl_11 = 0.05 * jax.random.normal(jax.random.fold_in(_tk, 500 + 11), (1250, 16), jnp.float32)
        tbl_12 = 0.05 * jax.random.normal(jax.random.fold_in(_tk, 500 + 12), (1000, 16), jnp.float32)
        tbl_13 = 0.05 * jax.random.normal(jax.random.fold_in(_tk, 500 + 13), (12500, 16), jnp.float32)
        tbl_14 = 0.05 * jax.random.normal(jax.random.fold_in(_tk, 500 + 14), (1000, 16), jnp.float32)
        tbl_15 = 0.05 * jax.random.normal(jax.random.fold_in(_tk, 500 + 15), (1000, 16), jnp.float32)
        tbl_16 = 0.05 * jax.random.normal(jax.random.fold_in(_tk, 500 + 16), (12500, 16), jnp.float32)
        tbl_17 = 0.05 * jax.random.normal(jax.random.fold_in(_tk, 500 + 17), (1250, 16), jnp.float32)
        tbl_18 = 0.05 * jax.random.normal(jax.random.fold_in(_tk, 500 + 18), (1000, 16), jnp.float32)
        tbl_19 = 0.05 * jax.random.normal(jax.random.fold_in(_tk, 500 + 19), (1250, 16), jnp.float32)
        tbl_20 = 0.05 * jax.random.normal(jax.random.fold_in(_tk, 500 + 20), (12500, 16), jnp.float32)
        tbl_21 = 0.05 * jax.random.normal(jax.random.fold_in(_tk, 500 + 21), (125000, 16), jnp.float32)
        tbl_22 = 0.05 * jax.random.normal(jax.random.fold_in(_tk, 500 + 22), (1000, 16), jnp.float32)
        tbl_23 = 0.05 * jax.random.normal(jax.random.fold_in(_tk, 500 + 23), (12500, 16), jnp.float32)
        tbl_24 = 0.05 * jax.random.normal(jax.random.fold_in(_tk, 500 + 24), (12500, 16), jnp.float32)
        tbl_25 = 0.05 * jax.random.normal(jax.random.fold_in(_tk, 500 + 25), (1250, 16), jnp.float32)
        tbl_26 = 0.05 * jax.random.normal(jax.random.fold_in(_tk, 500 + 26), (12500, 16), jnp.float32)
        tbl_27 = 0.05 * jax.random.normal(jax.random.fold_in(_tk, 500 + 27), (1250, 16), jnp.float32)
        tbl_28 = 0.05 * jax.random.normal(jax.random.fold_in(_tk, 500 + 28), (12500, 16), jnp.float32)
        tbl_29 = 0.05 * jax.random.normal(jax.random.fold_in(_tk, 500 + 29), (125000, 16), jnp.float32)
        tbl_30 = 0.05 * jax.random.normal(jax.random.fold_in(_tk, 500 + 30), (125000, 16), jnp.float32)
        tbl_31 = 0.05 * jax.random.normal(jax.random.fold_in(_tk, 500 + 31), (12500, 16), jnp.float32)
        tbl_32 = 0.05 * jax.random.normal(jax.random.fold_in(_tk, 500 + 32), (125000, 16), jnp.float32)
        tbl_33 = 0.05 * jax.random.normal(jax.random.fold_in(_tk, 500 + 33), (125000, 16), jnp.float32)
        tbl_34 = 0.05 * jax.random.normal(jax.random.fold_in(_tk, 500 + 34), (1250, 16), jnp.float32)
        tbl_35 = 0.05 * jax.random.normal(jax.random.fold_in(_tk, 500 + 35), (12500, 16), jnp.float32)
        tbl_36 = 0.05 * jax.random.normal(jax.random.fold_in(_tk, 500 + 36), (125000, 16), jnp.float32)
        tbl_37 = 0.05 * jax.random.normal(jax.random.fold_in(_tk, 500 + 37), (125000, 16), jnp.float32)
        tbl_38 = 0.05 * jax.random.normal(jax.random.fold_in(_tk, 500 + 38), (12500, 16), jnp.float32)
        _rk = jax.random.fold_in(_tk, 7)
        W_top1 = 0.0606339 * jax.random.normal(jax.random.fold_in(_tk, 801), (272, 512), jnp.float32)
        W_top2 = 0.0441942 * jax.random.normal(jax.random.fold_in(_tk, 802), (512, 256), jnp.float32)
        W_top3 = 0.0625 * jax.random.normal(jax.random.fold_in(_tk, 803), (256, 1), jnp.float32)
        b_top1 = jnp.zeros((512,), jnp.float32)
        b_top2 = jnp.zeros((256,), jnp.float32)
        return (dense_ctx, ids, tbl_0, tbl_1, tbl_2, tbl_3, tbl_4, tbl_5, tbl_6, tbl_7, tbl_8, tbl_9, tbl_10, tbl_11, tbl_12, tbl_13, tbl_14, tbl_15, tbl_16, tbl_17, tbl_18, tbl_19, tbl_20, tbl_21, tbl_22, tbl_23, tbl_24, tbl_25, tbl_26, tbl_27, tbl_28, tbl_29, tbl_30, tbl_31, tbl_32, tbl_33, tbl_34, tbl_35, tbl_36, tbl_37, tbl_38, W_top1, b_top1, W_top2, b_top2, W_top3)
    dense_ctx, ids, tbl_0, tbl_1, tbl_2, tbl_3, tbl_4, tbl_5, tbl_6, tbl_7, tbl_8, tbl_9, tbl_10, tbl_11, tbl_12, tbl_13, tbl_14, tbl_15, tbl_16, tbl_17, tbl_18, tbl_19, tbl_20, tbl_21, tbl_22, tbl_23, tbl_24, tbl_25, tbl_26, tbl_27, tbl_28, tbl_29, tbl_30, tbl_31, tbl_32, tbl_33, tbl_34, tbl_35, tbl_36, tbl_37, tbl_38, W_top1, b_top1, W_top2, b_top2, W_top3 = _rec_inputs()

    def _L0_rec_setup():
        import jax, jax.numpy as jnp
        import numpy as np
        B, F0, D = (256, 39, 16)
        LAYER_SIZES = [128, 128, 128]
        key = jax.random.key(seed)
        ks = jax.random.split(key, 1 + 2 * len(LAYER_SIZES))
        inputs = jax.random.normal(ks[0], (B, F0, D), dtype=jnp.float32)
        out = {'inputs': inputs}
        field_nums = [F0]
        for i, size in enumerate(LAYER_SIZES):
            fk = field_nums[-1]
            fan_in = F0 * fk
            scale = np.sqrt(2.0 / (fan_in + size)).astype(np.float32)
            out[f'w{i}'] = jax.random.normal(ks[1 + 2 * i], (F0, fk, size), dtype=jnp.float32) * scale
            out[f'b{i}'] = jnp.zeros((size,), dtype=jnp.float32)
            field_nums.append(size // 2)
        return out
    _L0_rec_all = _L0_rec_setup()
    _L0_rec_in = {k: v for k, v in _L0_rec_all.items() if k in ('w0', 'w1', 'w2', 'b0', 'b1', 'b2')}
    del _L0_rec_all
    return {'dense_ctx': dense_ctx, 'ids': ids, 'tbl_0': tbl_0, 'tbl_1': tbl_1, 'tbl_2': tbl_2, 'tbl_3': tbl_3, 'tbl_4': tbl_4, 'tbl_5': tbl_5, 'tbl_6': tbl_6, 'tbl_7': tbl_7, 'tbl_8': tbl_8, 'tbl_9': tbl_9, 'tbl_10': tbl_10, 'tbl_11': tbl_11, 'tbl_12': tbl_12, 'tbl_13': tbl_13, 'tbl_14': tbl_14, 'tbl_15': tbl_15, 'tbl_16': tbl_16, 'tbl_17': tbl_17, 'tbl_18': tbl_18, 'tbl_19': tbl_19, 'tbl_20': tbl_20, 'tbl_21': tbl_21, 'tbl_22': tbl_22, 'tbl_23': tbl_23, 'tbl_24': tbl_24, 'tbl_25': tbl_25, 'tbl_26': tbl_26, 'tbl_27': tbl_27, 'tbl_28': tbl_28, 'tbl_29': tbl_29, 'tbl_30': tbl_30, 'tbl_31': tbl_31, 'tbl_32': tbl_32, 'tbl_33': tbl_33, 'tbl_34': tbl_34, 'tbl_35': tbl_35, 'tbl_36': tbl_36, 'tbl_37': tbl_37, 'tbl_38': tbl_38, 'W_top1': W_top1, 'b_top1': b_top1, 'W_top2': W_top2, 'b_top2': b_top2, 'W_top3': W_top3, 'L0_rec_w0': _L0_rec_in['w0'], 'L0_rec_w1': _L0_rec_in['w1'], 'L0_rec_w2': _L0_rec_in['w2'], 'L0_rec_b0': _L0_rec_in['b0'], 'L0_rec_b1': _L0_rec_in['b1'], 'L0_rec_b2': _L0_rec_in['b2']}

def reference(dense_ctx, ids, tbl_0, tbl_1, tbl_2, tbl_3, tbl_4, tbl_5, tbl_6, tbl_7, tbl_8, tbl_9, tbl_10, tbl_11, tbl_12, tbl_13, tbl_14, tbl_15, tbl_16, tbl_17, tbl_18, tbl_19, tbl_20, tbl_21, tbl_22, tbl_23, tbl_24, tbl_25, tbl_26, tbl_27, tbl_28, tbl_29, tbl_30, tbl_31, tbl_32, tbl_33, tbl_34, tbl_35, tbl_36, tbl_37, tbl_38, W_top1, b_top1, W_top2, b_top2, W_top3, L0_rec_w0, L0_rec_w1, L0_rec_w2, L0_rec_b0, L0_rec_b1, L0_rec_b2):
    import jax
    import jax.numpy as jnp

    def _L0_rec_ref(inputs, w0, w1, w2, b0, b1, b2):
        import jax, jax.numpy as jnp
        import numpy as np
        B, F0, D = (256, 39, 16)
        LAYER_SIZES = [128, 128, 128]
        x0 = inputs
        xk = inputs
        params = [(w0, b0), (w1, b1), (w2, b2)]
        n_layers = len(params)
        direct = []
        for idx, (W, b) in enumerate(params):
            z = jnp.einsum('bhd,bkd,hks->bsd', x0, xk, W) + b[None, :, None]
            z = jax.nn.relu(z)
            if idx != n_layers - 1:
                half = z.shape[1] // 2
                xk = z[:, :half, :]
                direct.append(z[:, half:, :])
            else:
                direct.append(z)
        logit = jnp.sum(jnp.concatenate(direct, axis=1), axis=-1)
        return logit
    e = jnp.stack([tbl_0[ids[:, 0]], tbl_1[ids[:, 1]], tbl_2[ids[:, 2]], tbl_3[ids[:, 3]], tbl_4[ids[:, 4]], tbl_5[ids[:, 5]], tbl_6[ids[:, 6]], tbl_7[ids[:, 7]], tbl_8[ids[:, 8]], tbl_9[ids[:, 9]], tbl_10[ids[:, 10]], tbl_11[ids[:, 11]], tbl_12[ids[:, 12]], tbl_13[ids[:, 13]], tbl_14[ids[:, 14]], tbl_15[ids[:, 15]], tbl_16[ids[:, 16]], tbl_17[ids[:, 17]], tbl_18[ids[:, 18]], tbl_19[ids[:, 19]], tbl_20[ids[:, 20]], tbl_21[ids[:, 21]], tbl_22[ids[:, 22]], tbl_23[ids[:, 23]], tbl_24[ids[:, 24]], tbl_25[ids[:, 25]], tbl_26[ids[:, 26]], tbl_27[ids[:, 27]], tbl_28[ids[:, 28]], tbl_29[ids[:, 29]], tbl_30[ids[:, 30]], tbl_31[ids[:, 31]], tbl_32[ids[:, 32]], tbl_33[ids[:, 33]], tbl_34[ids[:, 34]], tbl_35[ids[:, 35]], tbl_36[ids[:, 36]], tbl_37[ids[:, 37]], tbl_38[ids[:, 38]]], axis=1)
    z = _L0_rec_ref(e, L0_rec_w0, L0_rec_w1, L0_rec_w2, L0_rec_b0, L0_rec_b1, L0_rec_b2)
    z = z.reshape(z.shape[0], -1)
    h = jnp.concatenate([z, dense_ctx], axis=1)
    h = jnp.maximum(h @ W_top1 + b_top1, 0.0)
    h = jnp.maximum(h @ W_top2 + b_top2, 0.0)
    y = h @ W_top3
    return y

_drawn_inputs = setup_inputs


def setup_inputs(seed=0):
    import zlib

    import numpy as np

    out = dict(_drawn_inputs(seed))
    spreads = {'b_top1': (0.0, 2.0),
     'b_top2': (0.0, 2.0),
     'L0_rec_b0': (0.0, 0.343),
     'L0_rec_b1': (0.0, 0.53),
     'L0_rec_b2': (0.0, 0.8)}
    factors = {'tbl_0': 8.0,
     'tbl_1': 8.0,
     'tbl_2': 8.0,
     'tbl_3': 8.0,
     'tbl_4': 8.0,
     'tbl_5': 8.0,
     'tbl_6': 8.0,
     'tbl_7': 8.0,
     'tbl_8': 8.0,
     'tbl_9': 8.0,
     'tbl_10': 8.0,
     'tbl_11': 8.0,
     'tbl_12': 8.0,
     'tbl_13': 8.0,
     'tbl_14': 8.0,
     'tbl_15': 8.0,
     'tbl_16': 8.0,
     'tbl_17': 8.0,
     'tbl_18': 8.0,
     'tbl_19': 8.0,
     'tbl_20': 8.0,
     'tbl_21': 8.0,
     'tbl_22': 8.0,
     'tbl_23': 8.0,
     'tbl_24': 8.0,
     'tbl_25': 8.0,
     'tbl_26': 8.0,
     'tbl_27': 8.0,
     'tbl_28': 8.0,
     'tbl_29': 8.0,
     'tbl_30': 8.0,
     'tbl_31': 8.0,
     'tbl_32': 8.0,
     'tbl_33': 8.0,
     'tbl_34': 8.0,
     'tbl_35': 8.0,
     'tbl_36': 8.0,
     'tbl_37': 8.0,
     'tbl_38': 8.0,
     'L0_rec_w0': 8.0,
     'L0_rec_w1': 6.23,
     'L0_rec_w2': 4.903,
     'dense_ctx': 8.0}
    for name, (base, spread) in spreads.items():
        noise = np.random.default_rng([zlib.crc32(name.encode()), seed]).standard_normal(out[name].shape)
        drawn = base * np.exp(spread * noise) if base else spread * noise
        out[name] = jnp.asarray(drawn.astype(out[name].dtype))
    for name, factor in factors.items():
        out[name] = (out[name] * factor).astype(out[name].dtype)
    return out
```

```python
import concourse.bass as bass
from concourse import mybir
from contextlib import ExitStack

BATCH, FIELDS, DIM = 1024, 39, 16
LAYER = 128
NEXT = LAYER // 2
GROUP = 128
GROUPS = BATCH // GROUP
BLOCK = GROUP // 2
COLS = BLOCK * DIM
BANK = 512
SHIFTS = FIELDS // 2 + 1
PER = 3
T0 = -(-SHIFTS // PER)
T1 = -(-FIELDS * NEXT // 128)
ROWS0 = PER * FIELDS
LAST0 = (SHIFTS - PER * (T0 - 1)) * FIELDS
WRAP = SHIFTS - 1
COPIES = 8
RING = 5
STEP = 2 * (T0 + 2 * T1)
QUADS = T1 // 4
TOP1, TOP2 = 512, 256


def rows0(t):
    return ROWS0 if t < T0 - 1 else LAST0


def rows1(t):
    return 128 if t < T1 - 1 else FIELDS * NEXT - 128 * (T1 - 1)


def build(nc, ids, tables, w0, w0t, w1, w2, b0, b1, b2, dense, wt1, bt1, wt2, bt2, wt3, out):
    f32 = mybir.dt.float32
    i32 = mybir.dt.int32
    ALU = mybir.AluOpType
    ACT = mybir.ActivationFunctionType
    AX = mybir.AxisListType

    scratch = nc.dram_tensor("x0_scratch", [GROUPS, FIELDS + WRAP, COPIES, 2 * COLS], f32, kind="Internal").ap()
    ROW = COPIES * 2 * COLS
    GRP = (FIELDS + WRAP) * ROW

    with ExitStack() as ctx:
        def sb(name, shape, dt=f32):
            return ctx.enter_context(nc.sbuf_tensor(name, shape, dt))

        def ps(name):
            return ctx.enter_context(nc.psum_tensor(name, [128, COLS], f32))

        def sem(name):
            return ctx.enter_context(nc.semaphore(name))

        ids_sb = sb("ids_sb", [GROUP, FIELDS], i32)
        emb = sb("emb", [GROUP, FIELDS * DIM])
        ident = sb("ident", [128, 128])
        x0T_top = sb("x0T_top", [128, 2 * COLS])
        x0T = x0T_top[0:FIELDS, :]
        x0_stack = sb("x0_stack", [ROWS0, COLS])
        x0_rot = sb("x0_rot", [ROWS0, T0, COLS])
        spread = sb("spread", [128, T1, COLS])
        prod = sb("prod", [128, RING, COLS])
        hid = [sb("hid0", [128, COLS]), sb("hid1", [128, COLS])]
        direct01 = sb("direct01", [128, COLS])
        direct2 = sb("direct2", [128, COLS])
        logit01 = sb("logit01", [128, BLOCK + BATCH])
        logit2 = sb("logit2", [128, BLOCK + BATCH])
        dense_sb = sb("dense_sb", [DIM, BATCH])
        w0_sb = sb("w0_sb", [ROWS0, T0, LAYER])
        w0t_sb = sb("w0t_sb", [ROWS0, T0, LAYER])
        w1_sb = sb("w1_sb", [128, T1, LAYER])
        w2_sb = sb("w2_sb", [128, T1, LAYER])
        bias = sb("bias", [LAYER, 3])
        wt1_sb = x0T_top[:, 0:2 * TOP1].rearrange("p (t n) -> p t n", t=2)
        wt2_sb = x0T_top[:, 2 * TOP1:].rearrange("p (t n) -> p t n", n=TOP2)
        wt1d_sb = sb("wt1d_sb", [DIM, TOP1])
        wt3_sb = sb("wt3_sb", [128, TOP2 // 128])
        bt1_sb = sb("bt1_sb", [128, TOP1 // 128])
        bt2_sb = sb("bt2_sb", [128, TOP2 // 128])
        z = [ps("z0"), ps("z1"), ps("z2")]
        xpose = ps("xpose")
        top1 = spread[:, 0:TOP1 // 128, :]
        top2 = spread[:, TOP1 // 128:TOP1 // 128 + TOP2 // 128, :]
        y_sb = spread[0:1, 6, :]

        ids_loaded = sem("ids_loaded")
        rows_gathered = sem("rows_gathered")
        ident_zero = sem("ident_zero")
        ident_ready = sem("ident_ready")
        half_transposed = sem("half_transposed")
        half_copied = sem("half_copied")
        scratch_written = sem("scratch_written")
        pairs_loaded = sem("pairs_loaded")
        spread_loaded = [sem(f"spread_loaded{q}") for q in range(QUADS)]
        w0_loaded = sem("w0_loaded")
        w0_cleared = sem("w0_cleared")
        w0_summed = sem("w0_summed")
        w1_loaded = sem("w1_loaded")
        w2_loaded = sem("w2_loaded")
        top_loaded = sem("top_loaded")
        bias_loaded = sem("bias_loaded")
        product_ready = sem("product_ready")
        product_used = sem("product_used")
        z_evacuated = [sem(f"z{l}_evacuated") for l in range(3)]
        direct2_cleared = sem("direct2_cleared")
        direct01_summed = sem("direct01_summed")
        direct2_summed = sem("direct2_summed")
        top1_done = sem("top1_done")
        top1_ready = sem("top1_ready")
        top2_done = sem("top2_done")
        top2_ready = sem("top2_ready")
        y_done = sem("y_done")
        y_ready = sem("y_ready")
        y_stored = sem("y_stored")

        block = ctx.enter_context(nc.Block())

        L1A, L0B, L2A = 0, T1, T1 + T0
        L1B, L0N = T0 + 2 * T1, T0 + 3 * T1
        L2B = L0N + T0
        LAST_L2B = L0N

        def first_tile(g):
            return T0 + g * STEP

        def each_group(eng, body):
            with eng.Fori(0, GROUPS - 1) as g:
                body(g, False)
            body(GROUPS - 1, True)

        @block.sync
        def _(sp):
            def load_weights(dst, src, done):
                full = T1 - 1
                sp.dma_start(dst[:, 0:full, :],
                             src[0:full * 128, :].rearrange("(t p) s -> p t s", p=128)).then_inc(done, 16)
                sp.dma_start(dst[0:rows1(full), full, :], src[full * 128:FIELDS * NEXT, :]).then_inc(done, 16)

            def write_scratch(g):
                sp.wait_ge(half_copied, 2 * g + 2)
                sp.dma_start(scratch[g, 0:FIELDS, :, :],
                             x0T.rearrange("p (o c) -> p o c", o=1).to_broadcast([FIELDS, COPIES, 2 * COLS])
                             ).then_inc(scratch_written, 16)
                sp.dma_start(scratch[g, FIELDS:FIELDS + WRAP, 0, :], x0T[0:WRAP, :]).then_inc(scratch_written, 16)

            def scratch_ap(g, offset, dims):
                return bass.AP(scratch.tensor, g * GRP + offset, dims)

            def load_pairs(g, half):
                for r in range(PER):
                    tiles = T0 if PER * (T0 - 1) + r < SHIFTS else T0 - 1
                    sp.dma_start(x0_stack[r * FIELDS:(r + 1) * FIELDS, :],
                                 scratch_ap(g, half * COLS, [[ROW, FIELDS], [1, COLS]])).then_inc(pairs_loaded, 16)
                    sp.dma_start(x0_rot[r * FIELDS:(r + 1) * FIELDS, 0:tiles, :],
                                 scratch_ap(g, r * ROW + half * COLS,
                                            [[ROW, FIELDS], [PER * ROW, tiles], [1, COLS]])
                                 ).then_inc(pairs_loaded, 16)

            def load_spread(g, half, t):
                n = rows1(t) // (128 // (2 * COPIES))
                sp.dma_start(spread[0:rows1(t), t, :],
                             scratch_ap(g, 2 * t * ROW + half * COLS,
                                        [[2 * COLS, n], [0, 128 // (2 * COPIES)], [1, COLS]])
                             ).then_inc(spread_loaded[t // 4], 16)

            sp.dma_start(w0_sb[:, 0:T0 - 1, :], w0[:, 0:T0 - 1, :]).then_inc(w0_loaded, 16)
            sp.dma_start(w0_sb[0:LAST0, T0 - 1, :], w0[0:LAST0, T0 - 1, :]).then_inc(w0_loaded, 16)
            sp.dma_start(w0t_sb[:, 1:T0 - 1, :], w0t[:, 1:T0 - 1, :]).then_inc(w0_loaded, 16)
            sp.dma_start(w0t_sb[0:LAST0, T0 - 1, :], w0t[0:LAST0, T0 - 1, :]).then_inc(w0_loaded, 16)
            sp.wait_ge(w0_cleared, 1)
            sp.dma_start(w0t_sb[FIELDS:ROWS0, 0, :], w0t[FIELDS:ROWS0, 0, :]).then_inc(w0_loaded, 16)
            for l, b in enumerate((b0, b1, b2)):
                sp.dma_start(bias[:, l:l + 1], b).then_inc(bias_loaded, 16)
            load_weights(w1_sb, w1, w1_loaded)
            load_weights(w2_sb, w2, w2_loaded)
            write_scratch(0)
            sp.wait_ge(scratch_written, 32)
            load_pairs(0, 0)
            for t in range(T1):
                load_spread(0, 0, t)

            def load_top():
                sp.dma_start(wt1_sb[0:NEXT, 0, :], wt1[NEXT:2 * NEXT, :]).then_inc(top_loaded, 16)
                sp.dma_start(wt1_sb[NEXT:128, 0, :], wt1[0:NEXT, :]).then_inc(top_loaded, 16)
                sp.dma_start(wt1_sb[:, 1, :], wt1[128:256, :]).then_inc(top_loaded, 16)
                sp.dma_start(wt1d_sb[:, :], wt1[256:256 + DIM, :]).then_inc(top_loaded, 16)
                sp.dma_start(wt2_sb[:, :, :], wt2.rearrange("(t p) n -> p t n", p=128)).then_inc(top_loaded, 16)
                sp.dma_start(wt3_sb[:, :], wt3).then_inc(top_loaded, 16)
                sp.dma_start(bt1_sb[:, :], bt1).then_inc(top_loaded, 16)
                sp.dma_start(bt2_sb[:, :], bt2).then_inc(top_loaded, 16)
                sp.dma_start(dense_sb[:, :], dense).then_inc(top_loaded, 16)

            def group(g, last):
                first = first_tile(g)
                sp.wait_ge(product_ready, first)
                load_pairs(g, 1)
                if last:
                    load_top()
                for t in range(T1):
                    sp.wait_ge(product_ready, first + L2A + t + 1)
                    load_spread(g, 1, t)
                if last:
                    return
                write_scratch(g + 1)
                sp.wait_ge(scratch_written, 32 * g + 64)
                load_pairs(g + 1, 0)
                for t in range(T1):
                    sp.wait_ge(product_ready, first + L2B + t + 1)
                    load_spread(g + 1, 0, t)

            each_group(sp, group)
            sp.wait_ge(y_ready, 1)
            sp.dma_start(out.rearrange("b o -> o b"), y_sb).then_inc(y_stored, 16)
            sp.wait_ge(y_stored, 16)

        @block.gpsimd
        def _(pool):
            ids_v = ids.rearrange("(g p) f -> g p f", p=GROUP)

            def load_ids(g):
                pool.dma_start(ids_sb[:, :], ids_v[g, :, :]).then_inc(ids_loaded, 16)

            def gather():
                for f in range(FIELDS):
                    pool.indirect_dma_start(
                        out=emb[:, f * DIM:(f + 1) * DIM], out_offset=None, in_=tables[f],
                        in_offset=bass.IndirectOffsetOnAxis(ap=ids_sb[:, f:f + 1], axis=0),
                    ).then_inc(rows_gathered, 16)

            load_ids(0)
            nc.gpsimd.memset(ident[:, :], 0.0).then_inc(ident_zero, 1)
            pool.wait_ge(ident_zero, 1)
            nc.gpsimd.affine_select(out=ident[:, :], in_=ident[:, :], compare_op=ALU.not_equal, fill=1.0, base=0,
                                    pattern=[[-1, 128]], channel_multiplier=1).then_inc(ident_ready, 1)
            pool.wait_ge(ids_loaded, 16)
            gather()
            with pool.Fori(1, GROUPS) as g:
                pool.wait_ge(rows_gathered, 16 * FIELDS * g)
                load_ids(g)
                pool.wait_ge(ids_loaded, 16 * g + 16)
                pool.wait_ge(half_transposed, 2 * g)
                pool.nop(nofuse=True)
                gather()

        @block.scalar
        def _(act):
            def copy_half(g, half, before=True):
                act.wait_ge(half_transposed, 2 * g + half + 1)
                if half == 0 and before:
                    act.wait_ge(scratch_written, 32 * g)
                dims = DIM // 2
                dst = x0T.rearrange("p (b d s) -> p b d s", b=2, d=DIM)[:, :, half * dims:(half + 1) * dims, :]
                src = xpose[0:FIELDS, :].rearrange("p (d b s) -> p b d s", d=dims, b=2)
                for b in range(2):
                    last = nc.scalar.activation(dst[:, b], src[:, b], ACT.Copy)
                last.then_inc(half_copied, 1)

            def relu(dst, src, l, lo, hi):
                return nc.scalar.activation(dst, src, ACT.Relu, bias=bias[lo:hi, l:l + 1])

            def evacuate0(n, end, before=True):
                act.wait_ge(product_used, end)
                relu(hid[0][0:NEXT, :], z[0][0:NEXT, :], 0, 0, NEXT)
                relu(hid[0][NEXT:128, :], z[0][0:NEXT, :], 0, 0, NEXT)
                if before:
                    act.wait_ge(direct01_summed, n)
                relu(direct01[NEXT:128, :], z[0][NEXT:128, :], 0, NEXT, 128).then_inc(z_evacuated[0], 1)

            def evacuate1(n, end):
                act.wait_ge(product_used, end)
                relu(hid[1][0:NEXT, :], z[1][NEXT:128, :], 1, NEXT, 128)
                relu(hid[1][NEXT:128, :], z[1][NEXT:128, :], 1, NEXT, 128)
                relu(direct01[0:NEXT, :], z[1][0:NEXT, :], 1, 0, NEXT).then_inc(z_evacuated[1], 1)

            def evacuate2(n, end):
                act.wait_ge(product_used, end)
                act.wait_ge(direct2_summed, n + 1)
                relu(direct2[:, :], z[2][:, :], 2, 0, 128).then_inc(z_evacuated[2], 1)

            for l in range(3):
                act.sem_inc(z_evacuated[l], 1)
            copy_half(0, 0, before=False)
            copy_half(0, 1)
            act.wait_ge(bias_loaded, 48)
            evacuate0(0, T0, before=False)

            def group(g, last):
                first = first_tile(g)
                evacuate1(2 * g, first + L1A + T1)
                evacuate0(2 * g + 1, first + L0B + T0)
                if not last:
                    copy_half(g + 1, 0)
                evacuate2(2 * g, first + L2A + T1)
                if not last:
                    copy_half(g + 1, 1)
                evacuate1(2 * g + 1, first + L1B + T1)
                if not last:
                    evacuate0(2 * g + 2, first + L0N + T0)
                evacuate2(2 * g + 1, first + (LAST_L2B if last else L2B) + T1)

            each_group(act, group)
            act.wait_ge(top_loaded, 9 * 16)
            for m in range(TOP1 // 128):
                act.wait_ge(top1_done, m + 1)
                nc.scalar.activation(top1[:, m, :], (z + [xpose])[m][:, :], ACT.Relu,
                                     bias=bt1_sb[:, m:m + 1]).then_inc(top1_ready, 1)
            for m in range(TOP2 // 128):
                act.wait_ge(top2_done, m + 1)
                nc.scalar.activation(top2[:, m, :], z[m][:, :], ACT.Relu,
                                     bias=bt2_sb[:, m:m + 1]).then_inc(top2_ready, 1)
            act.wait_ge(y_done, 1)
            nc.scalar.activation(y_sb, z[2][0:1, :], ACT.Copy).then_inc(y_ready, 1)

        @block.vector
        def _(dve):
            nc.vector.memset(w0t_sb[:, 0, :], 0.0).then_inc(w0_cleared, 1)
            nc.vector.memset(direct2[:, :], 0.0).then_inc(direct2_cleared, 1)
            dve.wait_ge(direct2_cleared, 1)
            dve.wait_ge(w0_loaded, 5 * 16)
            nc.vector.tensor_tensor(w0_sb[:, 0:T0 - 1, :], w0_sb[:, 0:T0 - 1, :], w0t_sb[:, 0:T0 - 1, :], ALU.add)
            nc.vector.tensor_tensor(w0_sb[0:LAST0, T0 - 1, :], w0_sb[0:LAST0, T0 - 1, :],
                                    w0t_sb[0:LAST0, T0 - 1, :], ALU.add).then_inc(w0_summed, 1)

            def product(dst_rows, slot, in0, in1):
                nc.vector.tensor_tensor(prod[0:dst_rows, slot, :], in0, in1, ALU.mult).then_inc(product_ready, 1)

            def ring_wait(first, j):
                dve.wait_ge(product_used, first + (j - 3 if j < 4 else j - 4))

            def layer0(n, first, at):
                dve.wait_ge(pairs_loaded, 2 * PER * 16 * (n + 1))
                for t in range(T0):
                    ring_wait(first, at + t)
                    r = rows0(t)
                    product(r, (at + t) % RING, x0_stack[0:r, :], x0_rot[0:r, t, :])

            def layer12(l, n, first, at):
                dve.wait_ge(z_evacuated[l - 1], n + 2)
                for t in range(T1):
                    if l == 1 and t % 4 == 0:
                        dve.wait_ge(spread_loaded[t // 4], 64 * (n + 1))
                    ring_wait(first, at + t)
                    r = rows1(t)
                    product(r, (at + t) % RING, spread[0:r, t, :], hid[l - 1][0:r, :])
                    if l == 1 and t == T1 // 2:
                        sum_direct2(n - 1)
                    if l == 2 and t == 0:
                        sum_direct01(n)

            def sum_over_d(dst, src, n):
                return nc.vector.tensor_reduce(dst[:, bass.ds(BLOCK * n + BLOCK, BLOCK)],
                                               src[:, :].rearrange("p (d s) -> p s d", d=DIM), AX.X, ALU.add)

            def sum_direct01(n):
                sum_over_d(logit01, direct01, n).then_inc(direct01_summed, 1)

            def sum_direct2(n):
                dve.wait_ge(z_evacuated[2], n + 2)
                sum_over_d(logit2, direct2, n).then_inc(direct2_summed, 1)

            dve.wait_ge(pairs_loaded, 2 * PER * 16)
            for t in range(T0):
                r = rows0(t)
                if t >= RING:
                    dve.wait_ge(product_used, t - RING + 1)
                product(r, (t + 3) % RING, x0_stack[0:r, :], x0_rot[0:r, t, :])

            def group(g, last):
                first = first_tile(g)
                layer12(1, 2 * g, first, L1A)
                layer0(2 * g + 1, first, L0B)
                layer12(2, 2 * g, first, L2A)
                layer12(1, 2 * g + 1, first, L1B)
                if not last:
                    layer0(2 * g + 2, first, L0N)
                layer12(2, 2 * g + 1, first, LAST_L2B if last else L2B)

            each_group(dve, group)
            sum_direct2(2 * GROUPS - 1)

        @block.tensor
        def _(pe):
            def transpose_half(g, half, before=True):
                if half == 0:
                    pe.wait_ge(rows_gathered, 16 * FIELDS * (g + 1))
                if before:
                    pe.wait_ge(half_copied, 2 * g + half)
                    pe.nop(nofuse=True)
                dims = DIM // 2
                rows = emb[:, :].rearrange("p (f d) -> p d f", d=DIM)
                for i in range(dims):
                    last = nc.tensor.transpose(xpose[0:FIELDS, i * GROUP:(i + 1) * GROUP],
                                               rows[:, half * dims + i, :], ident[:, :])
                last.then_inc(half_transposed, 1)

            def contract(l, weights, n, first, at, tiles, rows, shift=0):
                pe.wait_ge(z_evacuated[l], n + 1)
                for t in range(tiles):
                    pe.wait_ge(product_ready, first + at + t + 1)
                    r = rows(t)
                    for c in range(COLS // BANK):
                        last = nc.tensor.matmul(z[l][:, c * BANK:(c + 1) * BANK], weights[0:r, t, :],
                                                prod[0:r, (at + t + shift) % RING, c * BANK:(c + 1) * BANK],
                                                start=(t == 0), stop=(t == tiles - 1))
                    last.then_inc(product_used, 1)

            def layer(l, n, first, at, shift=0):
                weights, tiles, rows = ((w0_sb, T0, rows0), (w1_sb, T1, rows1), (w2_sb, T1, rows1))[l]
                contract(l, weights, n, first, at, tiles, rows, shift)

            pe.wait_ge(ident_ready, 1)
            transpose_half(0, 0, before=False)
            transpose_half(0, 1)
            pe.wait_ge(w0_summed, 1)
            layer(0, 0, 0, 0, shift=3)
            pe.wait_ge(w1_loaded, 32)
            pe.wait_ge(w2_loaded, 32)

            def group(g, last):
                first = first_tile(g)
                layer(1, 2 * g, first, L1A)
                layer(0, 2 * g + 1, first, L0B)
                if not last:
                    transpose_half(g + 1, 0)
                layer(2, 2 * g, first, L2A)
                if not last:
                    transpose_half(g + 1, 1)
                layer(1, 2 * g + 1, first, L1B)
                if not last:
                    layer(0, 2 * g + 2, first, L0N)
                layer(2, 2 * g + 1, first, LAST_L2B if last else L2B)

            each_group(pe, group)
            pe.wait_ge(top_loaded, 9 * 16)
            pe.wait_ge(direct01_summed, 2 * GROUPS)
            pe.wait_ge(direct2_summed, 2 * GROUPS + 1)
            halves = BATCH // BANK
            for m in range(TOP1 // 128):
                for c in range(halves):
                    acc = (z + [xpose])[m][:, c * BANK:(c + 1) * BANK]
                    ms = slice(m * 128, (m + 1) * 128)
                    samples = slice(BLOCK + c * BANK, BLOCK + (c + 1) * BANK)
                    nc.tensor.matmul(acc, wt1_sb[:, 0, ms], logit01[:, samples], start=True, stop=False)
                    nc.tensor.matmul(acc, wt1_sb[:, 1, ms], logit2[:, samples], start=False, stop=False)
                    last = nc.tensor.matmul(acc, wt1d_sb[:, ms], dense_sb[:, c * BANK:(c + 1) * BANK],
                                            start=False, stop=True)
                last.then_inc(top1_done, 1)
            for m in range(TOP2 // 128):
                for k in range(TOP1 // 128):
                    pe.wait_ge(top1_ready, max(k, m) + 1)
                    for c in range(halves):
                        last = nc.tensor.matmul(z[m][:, c * BANK:(c + 1) * BANK], wt2_sb[:, k, m * 128:(m + 1) * 128],
                                                top1[:, k, c * BANK:(c + 1) * BANK],
                                                start=(k == 0), stop=(k == TOP1 // 128 - 1))
                last.then_inc(top2_done, 1)
            for k in range(TOP2 // 128):
                pe.wait_ge(top2_ready, k + 1)
                for c in range(halves):
                    last = nc.tensor.matmul(z[2][0:1, c * BANK:(c + 1) * BANK], wt3_sb[:, k:k + 1],
                                            top2[:, k, c * BANK:(c + 1) * BANK],
                                            start=(k == 0), stop=(k == TOP2 // 128 - 1))
            last.then_inc(y_done, 1)


def kernel(**inputs):
    import numpy as np
    import concourse.bacc as bacc
    from concourse import mybir as mb
    from concourse.bass_utils import run_bass_kernel_spmd

    def a(name):
        return np.asarray(inputs[name])

    row = np.arange(ROWS0)[:, None]
    h = row % FIELDS
    k = (h + PER * np.arange(T0)[None, :] + row // FIELDS) % FIELDS
    w0 = a("L0_rec_w0")
    w1 = a("L0_rec_w1")
    b1 = a("L0_rec_b1")
    arrays = {
        "ids": a("ids"),
        "w0": w0[h, k],
        "w0t": w0[k, h],
        "w1": np.concatenate([w1[:, :, NEXT:], w1[:, :, :NEXT]], axis=2).reshape(FIELDS * NEXT, LAYER),
        "w2": a("L0_rec_w2").reshape(FIELDS * NEXT, LAYER),
        "b0": a("L0_rec_b0").reshape(LAYER, 1),
        "b1": np.concatenate([b1[NEXT:], b1[:NEXT]]).reshape(LAYER, 1),
        "b2": a("L0_rec_b2").reshape(LAYER, 1),
        "dense": a("dense_ctx").T,
        "wt1": a("W_top1"),
        "bt1": a("b_top1").reshape(TOP1 // 128, 128).T,
        "wt2": a("W_top2"),
        "bt2": a("b_top2").reshape(TOP2 // 128, 128).T,
        "wt3": a("W_top3").reshape(TOP2 // 128, 128).T,
    }
    for f in range(FIELDS):
        arrays[f"tbl_{f}"] = a(f"tbl_{f}")
    arrays = {n: np.ascontiguousarray(v) for n, v in arrays.items()}

    nc = bacc.Bacc("TRN2", target_bir_lowering=False, num_devices=1)
    t = {n: nc.dram_tensor(n, v.shape, mb.dt.from_np(v.dtype), kind="ExternalInput").ap() for n, v in arrays.items()}
    out = nc.dram_tensor("out", (BATCH, 1), mb.dt.float32, kind="ExternalOutput").ap()
    build(nc, t["ids"], [t[f"tbl_{f}"] for f in range(FIELDS)], t["w0"], t["w0t"], t["w1"], t["w2"],
          t["b0"], t["b1"], t["b2"], t["dense"], t["wt1"], t["bt1"], t["wt2"], t["bt2"], t["wt3"], out)
    r = run_bass_kernel_spmd(nc, [arrays], core_ids=[0])
    return r.results[0]["out"]
```

```python
import concourse.bass as bass
from concourse import mybir
from contextlib import ExitStack

BATCH, FIELDS, DIM = 1024, 39, 16
LAYER = 128
NEXT = LAYER // 2
BLOCK = 64
BLOCKS = BATCH // BLOCK
COLS = BLOCK * DIM
BANK = 512
PAIRS = (FIELDS + 1) // 2
SHIFTS = FIELDS // 2 + 1
PER = 3
T0 = -(-SHIFTS // PER)
T1 = -(-FIELDS * NEXT // 128)
ROWS0 = PER * FIELDS
LAST0 = (SHIFTS - PER * (T0 - 1)) * FIELDS
SROWS = FIELDS + SHIFTS - 1
COPIES = 8
STEP = 2 * T1 + T0
QUADS = T1 // 4
TOP1, TOP2 = 512, 256
HALF = DIM // 2

KINDS = ["GFDGDFF", "GFDGF" * 4, "GFDGF" * 4]
TILES = [len(k) for k in KINDS]
SPLITS = [[t for t, k in enumerate(ks) if k != "F"] for ks in KINDS]
FULLS = [[t for t, k in enumerate(ks) if k == "F"] for ks in KINDS]
SPLIT_AT = [0, len(SPLITS[0]), len(SPLITS[0]) + len(SPLITS[1])]
FULL_AT = [0, len(FULLS[0]), len(FULLS[0]) + len(FULLS[1])]
N_SPLIT = sum(map(len, SPLITS))
N_FULL = sum(map(len, FULLS))
PRODS, PARTS = 6, 4

ORDER = [(1, t) for t in range(T1)] + [(0, t) for t in range(T0)] + [(2, t) for t in range(T1)]
L1, L0, L2 = 0, T1, T1 + T0
KIND = [KINDS[l][t] for l, t in ORDER]


def rows(l, t):
    if l == 0:
        return ROWS0 if t < T0 - 1 else LAST0
    return 128 if t < T1 - 1 else FIELDS * NEXT - 128 * (T1 - 1)


PROLOGUE = -1
LAST = BLOCKS - 1


def is_step(n, m):
    return isinstance(n, int) and n == m


def executed(n):
    js = range(L0, L2) if is_step(n, PROLOGUE) else range(STEP)
    return [j for j in js if not (is_step(n, LAST) and L0 <= j < L2)]


def reached(n, j, kinds):
    of_step = sum(k in kinds for k in KIND)
    if is_step(n, PROLOGUE):
        return sum(KIND[i] in kinds for i in range(L0, j + 1))
    prologue = sum(k in kinds for k in KINDS[0])
    if j < 0:
        return n * of_step + prologue - sum(k in kinds for k in KIND[STEP + j + 1:])
    return n * of_step + prologue + sum(KIND[i] in kinds for i in executed(n) if i <= j)


def earlier(n, j):
    return [i for i in reversed(executed(n)) if i < j] + list(range(-1, -STEP - 1, -1))


def product_slot(j):
    return j % PRODS


def product_before(n, j):
    return next(i for i in earlier(n, j) if product_slot(i % STEP) == product_slot(j))


def part_slot(j):
    return sum(k != "F" for k in KIND[:j]) % PARTS


def parts_before(n, j):
    return next(i for i in earlier(n, j) if KIND[i] != "F" and part_slot(i % STEP) == part_slot(j))


def build(nc, ids, base, table, w0, w0t, w1, w2, b0, b1, b2, dense, wt1, bt1, wt2, bt2, wt3, out):
    f32, f32r, i32 = mybir.dt.float32, mybir.dt.float32r, mybir.dt.int32
    ALU = mybir.AluOpType
    ACT = mybir.ActivationFunctionType
    AX = mybir.AxisListType

    scratch = nc.dram_tensor("x0_scratch", [BLOCKS, SROWS, COPIES, COLS], f32, kind="Internal").ap()
    ROW = COPIES * COLS

    with ExitStack() as ctx:
        def sb(name, shape, dt=f32):
            return ctx.enter_context(nc.sbuf_tensor(name, shape, dt))

        def ps(name):
            return ctx.enter_context(nc.psum_tensor(name, [128, COLS], f32))

        def sem(name):
            return ctx.enter_context(nc.semaphore(name))

        rows_idx = sb("rows_idx", [128, BLOCKS * PAIRS], i32)
        base_sb = sb("base_sb", [128, BLOCKS * PAIRS], i32)
        block_idx = [sb(f"block_idx{p}", [128, PAIRS], i32) for p in range(2)]
        emb = [sb(f"emb{p}", [128, PAIRS * DIM]) for p in range(2)]
        ident = sb("ident", [128, 128])
        x0T = sb("x0T", [PAIRS, 2, COLS])
        x0_stack = sb("x0_stack", [ROWS0, COLS])
        x0_rot = sb("x0_rot", [128, T0, COLS])
        spread = sb("spread", [128, T1, COLS])
        prod_at = nc.sbuf_base
        prod = sb("prod", [128, PRODS, COLS])
        lo = nc.alloc_sbuf_tensor_at("lo", [128, PRODS, COLS], f32r, offset=prod_at)
        hi = sb("hi", [128, PARTS, COLS], f32r)
        direct01 = sb("direct01", [128, COLS])
        direct2 = sb("direct2", [128, COLS])
        logit01 = sb("logit01", [128, BLOCK + BATCH])
        logit2 = sb("logit2", [128, BLOCK + BATCH])
        wfull = sb("wfull", [128, N_FULL, LAYER])
        whi = sb("whi", [128, N_SPLIT, LAYER], f32r)
        wlo = sb("wlo", [128, N_SPLIT, LAYER], f32r)
        bias = sb("bias", [LAYER, 3])
        wt3_sb = sb("wt3_sb", [128, TOP2 // 128])
        bt1_sb = sb("bt1_sb", [128, TOP1 // 128])
        bt2_sb = sb("bt2_sb", [128, TOP2 // 128])
        acc = [ps("acc0"), ps("acc1")]
        xk = [ps("xk0"), ps("xk1")]

        STAGED = 5
        stage = spread[:, T1 - STAGED:T1, :].rearrange("p t c -> p (t c)").rearrange("p (w s) -> p w s", s=LAYER)
        w_stage = stage[:, 0:N_SPLIT, :]
        w0f_stage = stage[:, N_SPLIT:N_SPLIT + len(FULLS[0]), :]
        w0t_stage = stage[:, N_SPLIT + len(FULLS[0]):N_SPLIT + len(FULLS[0]) + T0, :]
        wt1_sb = x0_rot[:, 0, :].rearrange("p (t n) -> p t n", n=TOP1)
        wt2_sb = x0_rot[:, 1, :].rearrange("p (t n) -> p t n", n=TOP2)
        dense_sb = x0_rot[0:DIM, 2, 0:BATCH]
        wt1d_sb = x0_rot[0:DIM, 3, 0:TOP1]
        top1 = spread[:, 0:TOP1 // 128, :]
        top2 = spread[:, TOP1 // 128:TOP1 // 128 + TOP2 // 128, :]
        y_sb = spread[0:1, 6, :]

        ids_loaded = sem("ids_loaded")
        idx_added = sem("idx_added")
        idx_ready = sem("idx_ready")
        rows_gathered = [sem(f"rows_gathered{p}") for p in range(2)]
        ident_zero = sem("ident_zero")
        ident_ready = sem("ident_ready")
        half_transposed = sem("half_transposed")
        half_copied = sem("half_copied")
        first_written = sem("first_written")
        replicas_written = sem("replicas_written")
        pairs_loaded = sem("pairs_loaded")
        spread_loaded = [sem(f"spread_loaded{q}") for q in range(QUADS)]
        w0_loaded = sem("w0_loaded")
        w0_cleared = sem("w0_cleared")
        w0_summed = sem("w0_summed")
        w12_loaded = sem("w12_loaded")
        whi_ready = sem("whi_ready")
        wlo_ready = sem("wlo_ready")
        top_loaded = sem("top_loaded")
        bias_loaded = sem("bias_loaded")
        product_ready = sem("product_ready")
        hi_ready = sem("hi_ready")
        lo_ready_d = sem("lo_ready_d")
        lo_ready_g = sem("lo_ready_g")
        tile_used = sem("tile_used")
        xk1_ready = sem("xk1_ready")
        z_evacuated = [sem(f"z{l}_evacuated") for l in range(3)]
        direct2_cleared = sem("direct2_cleared")
        direct01_summed = sem("direct01_summed")
        direct2_summed = sem("direct2_summed")
        top1_done = sem("top1_done")
        top1_ready = sem("top1_ready")
        top2_done = sem("top2_done")
        top2_ready = sem("top2_ready")
        y_done = sem("y_done")
        y_ready = sem("y_ready")
        y_stored = sem("y_stored")

        block = ctx.enter_context(nc.Block())

        def each_step(eng, step):
            with eng.Fori(0, BLOCKS // 2 - 1) as g:
                step(2 * g, 0)
                step(2 * g + 1, 1)
            step(LAST - 1, 0)
            step(LAST, 1)

        def past_end(n, ahead):
            return isinstance(n, int) and n + ahead > LAST

        def accumulator(l, parity):
            return acc[1 - parity if l == 0 else parity]

        @block.sync
        def _(sp):
            def load_weights():
                n = len(SPLITS[0])
                sp.dma_start(w_stage[0:ROWS0, 0:n, :], w0[:, 0:n, :]).then_inc(w0_loaded, 16)
                sp.dma_start(w0f_stage[0:ROWS0, 0:len(FULLS[0]) - 1, :], w0[:, n:T0 - 1, :]).then_inc(w0_loaded, 16)
                sp.dma_start(w0f_stage[0:LAST0, len(FULLS[0]) - 1, :], w0[0:LAST0, T0 - 1, :]).then_inc(w0_loaded, 16)
                sp.dma_start(w0t_stage[0:ROWS0, 1:T0 - 1, :], w0t[:, 1:T0 - 1, :]).then_inc(w0_loaded, 16)
                sp.dma_start(w0t_stage[0:LAST0, T0 - 1, :], w0t[0:LAST0, T0 - 1, :]).then_inc(w0_loaded, 16)
                sp.wait_ge(w0_cleared, 1)
                sp.dma_start(w0t_stage[FIELDS:ROWS0, 0, :], w0t[FIELDS:ROWS0, 0, :]).then_inc(w0_loaded, 16)
                for l, b in enumerate((b0, b1, b2)):
                    sp.dma_start(bias[:, l:l + 1], b).then_inc(bias_loaded, 16)
                for l, w in ((1, w1), (2, w2)):
                    n, f = len(SPLITS[l]), len(FULLS[l]) - 1
                    sp.dma_start(w_stage[:, SPLIT_AT[l]:SPLIT_AT[l] + n, :],
                                 w[0:n * 128, :].rearrange("(t p) s -> p t s", p=128)).then_inc(w12_loaded, 16)
                    sp.dma_start(wfull[:, FULL_AT[l]:FULL_AT[l] + f, :],
                                 w[n * 128:(n + f) * 128, :].rearrange("(t p) s -> p t s", p=128)
                                 ).then_inc(w12_loaded, 16)
                    sp.dma_start(wfull[0:rows(l, T1 - 1), FULL_AT[l] + f, :],
                                 w[(n + f) * 128:FIELDS * NEXT, :]).then_inc(w12_loaded, 16)

            def load_top():
                sp.dma_start(wt1_sb[0:NEXT, 0, :], wt1[NEXT:2 * NEXT, :]).then_inc(top_loaded, 16)
                sp.dma_start(wt1_sb[NEXT:128, 0, :], wt1[0:NEXT, :]).then_inc(top_loaded, 16)
                sp.dma_start(wt1_sb[:, 1, :], wt1[128:256, :]).then_inc(top_loaded, 16)
                sp.dma_start(wt1d_sb, wt1[256:256 + DIM, :]).then_inc(top_loaded, 16)
                sp.dma_start(wt2_sb, wt2.rearrange("(t p) n -> p t n", p=128)).then_inc(top_loaded, 16)
                sp.dma_start(wt3_sb[:, :], wt3).then_inc(top_loaded, 16)
                sp.dma_start(bt1_sb[:, :], bt1).then_inc(top_loaded, 16)
                sp.dma_start(bt2_sb[:, :], bt2).then_inc(top_loaded, 16)
                sp.dma_start(dense_sb, dense).then_inc(top_loaded, 16)

            def write_first(m):
                sp.wait_ge(half_copied, 2 * m + 2)
                sp.nop(nofuse=True)
                for p in range(2):
                    sp.dma_start(scratch[m, p * PAIRS:(p + 1) * PAIRS, 0, :], x0T[:, p, :]).then_inc(first_written, 16)
                sp.dma_start(scratch[m, FIELDS + 1:SROWS, 0, :],
                             x0T[1:SROWS - FIELDS, 0, :]).then_inc(first_written, 16)

            def write_replicas(m):
                for p in range(2):
                    sp.dma_start(scratch[m, p * PAIRS:(p + 1) * PAIRS, 1:COPIES, :],
                                 x0T[:, p:p + 1, :].to_broadcast([PAIRS, COPIES - 1, COLS])
                                 ).then_inc(replicas_written, 16)

            def scratch_ap(m, offset, dims):
                return bass.AP(scratch.tensor, m * (SROWS * ROW) + offset, dims)

            def load_pairs(m):
                sp.wait_ge(first_written, 48 * m + 48)
                sp.nop(nofuse=True)
                for r in range(PER):
                    tiles = T0 if PER * (T0 - 1) + r < SHIFTS else T0 - 1
                    sp.dma_start(x0_stack[r * FIELDS:(r + 1) * FIELDS, :],
                                 scratch_ap(m, 0, [[ROW, FIELDS], [1, COLS]])).then_inc(pairs_loaded, 16)
                    sp.dma_start(x0_rot[r * FIELDS:(r + 1) * FIELDS, 0:tiles, :],
                                 scratch_ap(m, r * ROW, [[ROW, FIELDS], [PER * ROW, tiles], [1, COLS]])
                                 ).then_inc(pairs_loaded, 16)

            def load_spread(m, t):
                n = rows(1, t) // (128 // (2 * COPIES))
                sp.dma_start(spread[0:rows(1, t), t, :],
                             scratch_ap(m, 2 * t * ROW, [[COLS, n], [0, 128 // (2 * COPIES)], [1, COLS]])
                             ).then_inc(spread_loaded[t // 4], 16)

            sp.dma_start(rows_idx[:, :], ids).then_inc(ids_loaded, 16)
            sp.dma_start(base_sb[:, :], base).then_inc(ids_loaded, 16)
            load_weights()
            write_first(0)
            load_pairs(0)
            write_replicas(0)
            sp.wait_ge(replicas_written, 32)
            for t in range(T1):
                if t == T1 - STAGED:
                    sp.wait_ge(wlo_ready, 3)
                load_spread(0, t)
            write_first(1)
            sp.wait_ge(product_ready, T0)
            load_pairs(1)
            write_replicas(1)

            def step(n, parity):
                if not past_end(n, 2):
                    write_first(n + 2)
                if not past_end(n, 1):
                    sp.wait_ge(replicas_written, 32 * n + 64)
                    sp.nop(nofuse=True)
                    for t in range(T1):
                        sp.wait_ge(product_ready, reached(n, L2 + t, "FDG"))
                        load_spread(n + 1, t)
                if not past_end(n, 2):
                    load_pairs(n + 2)
                    write_replicas(n + 2)
                elif not past_end(n, 1):
                    load_top()

            each_step(sp, step)
            sp.wait_ge(y_ready, 2)
            sp.dma_start(out.rearrange("b o -> o b"), y_sb).then_inc(y_stored, 16)
            sp.wait_ge(y_stored, 16)

        @block.gpsimd
        def _(pool):
            def take_indices(m, parity, reuse=True):
                if reuse:
                    pool.wait_ge(rows_gathered[parity], 8 * PAIRS * (m - parity))
                pool.nop(nofuse=True)
                nc.gpsimd.tensor_copy(block_idx[parity][:, :], rows_idx[:, bass.ds(m * PAIRS, PAIRS)]
                                      ).then_inc(idx_ready, 1)
                pool.wait_ge(idx_ready, m + 1)
                if reuse:
                    pool.wait_ge(half_transposed, 2 * m - 2)
                pool.nop(nofuse=True)

            def gather(parity, start, stop):
                for i in range(start, stop):
                    pool.indirect_dma_start(
                        out=emb[parity][:, i * DIM:(i + 1) * DIM], out_offset=None, in_=table,
                        in_offset=bass.IndirectOffsetOnAxis(ap=block_idx[parity][:, i:i + 1], axis=0),
                    ).then_inc(rows_gathered[parity], 16)

            def subtract(n, j):
                r = rows(*ORDER[j])
                pool.wait_ge(hi_ready, reached(n, j, "DG"))
                nc.gpsimd.tensor_tensor(lo[0:r, product_slot(j), :], prod[0:r, product_slot(j), :],
                                        hi[0:r, part_slot(j), :].bitcast(f32), ALU.subtract).then_inc(lo_ready_g, 1)

            nc.gpsimd.memset(ident[:, :], 0.0).then_inc(ident_zero, 1)
            pool.wait_ge(ids_loaded, 32)
            nc.gpsimd.tensor_tensor(rows_idx[:, :], rows_idx[:, :], base_sb[:, :], ALU.add).then_inc(idx_added, 1)
            pool.wait_ge(idx_added, 1)
            take_indices(0, 0, reuse=False)
            gather(0, 0, PAIRS)
            pool.wait_ge(ident_zero, 1)
            nc.gpsimd.affine_select(out=ident[:, :], in_=ident[:, :], compare_op=ALU.not_equal, fill=1.0, base=0,
                                    pattern=[[-1, 128]], channel_multiplier=1).then_inc(ident_ready, 1)
            take_indices(1, 1, reuse=False)
            gather(1, 0, PAIRS)
            take_indices(2, 0)

            def layer(n, l, m=None, parity=0, gathers=(0, 0)):
                at, tiles = (L0, L1, L2)[l], [t for t, k in enumerate(KINDS[l]) if k == "G"]
                start, stop = gathers
                between = max(1, len(tiles) - (2 if l == 1 else 0))
                for i, t in enumerate(tiles):
                    subtract(n, at + t)
                    if m is not None and i < between:
                        gather(parity, start + i * (stop - start) // between,
                               start + (i + 1) * (stop - start) // between)

            GATHERS = {0: (0, 4), 2: (4, 12), 1: (12, PAIRS)}
            layer(PROLOGUE, 0, 2, 0, GATHERS[0])
            gather(0, *GATHERS[2])
            layer(0, 1, 2, 0, GATHERS[1])

            def step(n, parity):
                m = None if past_end(n, 3) else n + 3
                if m is not None:
                    take_indices(m, 1 - parity)
                if not past_end(n, 1):
                    layer(n, 0, m, 1 - parity, GATHERS[0])
                layer(n, 2, m, 1 - parity, GATHERS[2])
                if not past_end(n, 1):
                    layer(n + 1, 1, m, 1 - parity, GATHERS[1])

            with pool.Fori(0, (BLOCKS - 3) // 2) as g:
                step(2 * g, 0)
                step(2 * g + 1, 1)
            for n in range((BLOCKS - 3) // 2 * 2, BLOCKS):
                step(n, n % 2)

        @block.scalar
        def _(act):
            def copy_half(m, half, source, reuse=True):
                act.wait_ge(half_transposed, 2 * m + half + 1)
                if half == 0 and reuse:
                    act.wait_ge(first_written, 48 * m)
                    act.wait_ge(replicas_written, 32 * m)
                dst = x0T[:, :, half * HALF * BLOCK:(half + 1) * HALF * BLOCK].rearrange("i p (d s) -> i p d s", s=BLOCK)
                src = source[0:PAIRS, :].rearrange("i (d p s) -> i p d s", p=2, s=BLOCK)
                nc.scalar.activation(dst, src, ACT.Copy).then_inc(half_copied, 1)

            def relu(dst, src, l, first, last):
                return nc.scalar.activation(dst, src, ACT.Relu, bias=bias[first:last, l:l + 1])

            def evacuate(l, m, z, done, copied=None, reuse=True):
                if copied is not None:
                    act.wait_ge(half_copied, copied)
                act.wait_ge(tile_used, done)
                if l == 0:
                    relu(xk[0][0:NEXT, :], z[0:NEXT, :], 0, 0, NEXT)
                    relu(xk[0][NEXT:128, :], z[0:NEXT, :], 0, 0, NEXT)
                    if reuse:
                        act.wait_ge(direct01_summed, m)
                    last = relu(direct01[NEXT:128, :], z[NEXT:128, :], 0, NEXT, 128)
                elif l == 1:
                    relu(xk[1][0:NEXT, :], z[NEXT:128, :], 1, NEXT, 128)
                    relu(xk[1][NEXT:128, :], z[NEXT:128, :], 1, NEXT, 128).then_inc(xk1_ready, 1)
                    return
                else:
                    act.wait_ge(direct2_summed, m + 1)
                    last = relu(direct2[:, :], z[:, :], 2, 0, 128)
                last.then_inc(z_evacuated[l], 1)

            def evacuate_direct1(z):
                relu(direct01[0:NEXT, :], z[0:NEXT, :], 1, 0, NEXT).then_inc(z_evacuated[1], 1)

            def round_hi(n, start, stop):
                for j in range(start, stop):
                    if KIND[j] != "F":
                        r = rows(*ORDER[j])
                        act.wait_ge(product_ready, reached(n, j, "FDG"))
                        if not is_step(n, PROLOGUE):
                            act.wait_ge(tile_used, reached(n, parts_before(n, j), "FDG"))
                        nc.scalar.activation(hi[0:r, part_slot(j), :], prod[0:r, product_slot(j), :],
                                             ACT.Copy).then_inc(hi_ready, 1)

            act.sem_inc(z_evacuated[2], 1)
            for l in range(3):
                act.wait_ge((w0_summed, w12_loaded, w12_loaded)[l], (1, 96, 96)[l])
                n, r = len(SPLITS[l]), rows(l, 0)
                nc.scalar.activation(whi[0:r, SPLIT_AT[l]:SPLIT_AT[l] + n, :],
                                     w_stage[0:r, SPLIT_AT[l]:SPLIT_AT[l] + n, :], ACT.Copy).then_inc(whi_ready, 1)
            act.wait_ge(bias_loaded, 48)
            copy_half(0, 0, xk[0], reuse=False)
            copy_half(0, 1, xk[1])
            round_hi(PROLOGUE, L0, L2)
            evacuate(0, 0, accumulator(0, 1), T0, copied=2, reuse=False)
            copy_half(1, 0, xk[1])
            copy_half(1, 1, xk[1])
            XK1_AFTER, DIRECT1_AFTER, COPY0_AFTER = 3, 4, 5
            COPY1_AFTER, Z0_AFTER, Z2_AFTER = 4, 5, 4
            round_hi(0, L1, L1 + Z2_AFTER)

            def step(n, parity):
                z1, z0, z2 = (accumulator(l, parity) for l in (1, 0, 2))
                round_hi(n, L1 + Z2_AFTER, L0)
                if past_end(n, 1):
                    evacuate(1, n, z1, reached(n, L0 - 1, "FDG"))
                    evacuate_direct1(z1)
                    round_hi(n, L2, STEP)
                    evacuate(2, n, z2, reached(n, STEP - 1, "FDG"))
                    return
                round_hi(n, L0, L0 + XK1_AFTER)
                evacuate(1, n, z1, reached(n, L0 - 1, "FDG"), copied=4)
                round_hi(n, L0 + XK1_AFTER, L0 + DIRECT1_AFTER)
                evacuate_direct1(z1)
                round_hi(n, L0 + DIRECT1_AFTER, L0 + COPY0_AFTER)
                if not past_end(n, 2):
                    copy_half(n + 2, 0, xk[0])
                round_hi(n, L0 + COPY0_AFTER, L2 + COPY1_AFTER)
                if not past_end(n, 2):
                    copy_half(n + 2, 1, xk[0])
                round_hi(n, L2 + COPY1_AFTER, L2 + Z0_AFTER)
                evacuate(0, n + 1, z0, reached(n, L2 - 1, "FDG"), copied=None if past_end(n, 2) else 2 * n + 6)
                round_hi(n, L2 + Z0_AFTER, STEP)
                round_hi(n + 1, L1, L1 + Z2_AFTER)
                evacuate(2, n, z2, reached(n, STEP - 1, "FDG"))

            each_step(act, step)
            act.wait_ge(top_loaded, 9 * 16)
            halves = BATCH // BANK
            for c in range(halves):
                cols = slice(c * BANK, (c + 1) * BANK)
                for m in range(TOP1 // 128):
                    act.wait_ge(top1_done, c * (TOP1 // 128) + m + 1)
                    nc.scalar.activation(top1[:, m, cols], (acc + xk)[m][:, cols], ACT.Relu,
                                         bias=bt1_sb[:, m:m + 1]).then_inc(top1_ready, 1)
            for c in range(halves):
                cols = slice(c * BANK, (c + 1) * BANK)
                for m in range(TOP2 // 128):
                    act.wait_ge(top2_done, c * (TOP2 // 128) + m + 1)
                    nc.scalar.activation(top2[:, m, cols], acc[m][:, cols], ACT.Relu,
                                         bias=bt2_sb[:, m:m + 1]).then_inc(top2_ready, 1)
            for c in range(halves):
                cols = slice(c * BANK, (c + 1) * BANK)
                act.wait_ge(y_done, c + 1)
                nc.scalar.activation(y_sb[:, cols], xk[0][0:1, cols], ACT.Copy).then_inc(y_ready, 1)

        @block.vector
        def _(dve):
            nc.vector.memset(w0t_stage[:, 0, :], 0.0).then_inc(w0_cleared, 1)
            nc.vector.memset(direct2[:, :], 0.0).then_inc(direct2_cleared, 1)
            dve.wait_ge(direct2_cleared, 1)
            dve.wait_ge(w0_loaded, 6 * 16)
            n, f = len(SPLITS[0]), len(FULLS[0])
            nc.vector.tensor_tensor(wfull[0:ROWS0, 0:f - 1, :], w0f_stage[0:ROWS0, 0:f - 1, :],
                                    w0t_stage[0:ROWS0, n:T0 - 1, :], ALU.add)
            nc.vector.tensor_tensor(wfull[0:LAST0, f - 1, :], w0f_stage[0:LAST0, f - 1, :],
                                    w0t_stage[0:LAST0, T0 - 1, :], ALU.add)
            nc.vector.tensor_tensor(w_stage[0:ROWS0, 0:n, :], w_stage[0:ROWS0, 0:n, :],
                                    w0t_stage[0:ROWS0, 0:n, :], ALU.add).then_inc(w0_summed, 1)
            dve.wait_ge(w0_summed, 1)
            for l in range(3):
                dve.wait_ge(whi_ready, l + 1)
                part = slice(SPLIT_AT[l], SPLIT_AT[l] + len(SPLITS[l]))
                r = rows(l, 0)
                nc.vector.tensor_tensor(wlo[0:r, part, :], w_stage[0:r, part, :], whi[0:r, part, :].bitcast(f32),
                                        ALU.subtract).then_inc(wlo_ready, 1)

            def product(n, j):
                l, t = ORDER[j]
                r = rows(l, t)
                if not is_step(n, PROLOGUE) or j - L0 >= PRODS:
                    dve.wait_ge(tile_used, reached(n, product_before(n, j), "FDG"))
                in0, in1 = (x0_stack[0:r, :], x0_rot[0:r, t, :]) if l == 0 else (spread[0:r, t, :], xk[l - 1][0:r, :])
                nc.vector.tensor_tensor(prod[0:r, product_slot(j), :], in0, in1, ALU.mult).then_inc(product_ready, 1)

            def subtract(n, j):
                r = rows(*ORDER[j])
                dve.wait_ge(hi_ready, reached(n, j, "DG"))
                nc.vector.tensor_tensor(lo[0:r, product_slot(j), :], prod[0:r, product_slot(j), :],
                                        hi[0:r, part_slot(j), :].bitcast(f32), ALU.subtract).then_inc(lo_ready_d, 1)

            DELAY = 2

            def tiles(n, start, stop):
                for j in range(start, stop):
                    l, t = ORDER[j]
                    if l == 0 and t == 0:
                        dve.wait_ge(pairs_loaded, 2 * PER * 16 * (n + 2))
                    if l > 0 and t == 0:
                        dve.wait_ge(z_evacuated[0] if l == 1 else xk1_ready, n + 1)
                    if l == 1 and t % 4 == 0:
                        dve.wait_ge(spread_loaded[t // 4], 64 * n + 64)
                    product(n, j)
                    if j - DELAY >= start and KIND[j - DELAY] == "D":
                        subtract(n, j - DELAY)
                    if l == 1 and t == T1 // 2:
                        sum_direct2(n)
                    if l == 2 and t == 3:
                        dve.wait_ge(z_evacuated[1], n + 1)
                        sum_direct01(n)
                for j in range(stop - DELAY, stop):
                    if KIND[j] == "D":
                        subtract(n, j)

            def sum_over_d(dst, src, column):
                return nc.vector.tensor_reduce(dst[:, bass.ds(column, BLOCK)],
                                               src[:, :].rearrange("p (d s) -> p s d", d=DIM), AX.X, ALU.add)

            def sum_direct01(m):
                sum_over_d(logit01, direct01, BLOCK * m + BLOCK).then_inc(direct01_summed, 1)

            def sum_direct2(n):
                dve.wait_ge(z_evacuated[2], n + 1)
                sum_over_d(logit2, direct2, BLOCK * n).then_inc(direct2_summed, 1)

            tiles(PROLOGUE, L0, L2)

            def step(n, parity):
                if past_end(n, 1):
                    tiles(n, L1, L0)
                    tiles(n, L2, STEP)
                else:
                    tiles(n, L1, STEP)

            each_step(dve, step)
            sum_direct2(BLOCKS)

        @block.tensor
        def _(pe):
            def transpose_half(m, parity, half, target, reuse=True):
                if half == 0:
                    pe.wait_ge(rows_gathered[parity], 8 * PAIRS * (m + 2 - parity))
                if reuse:
                    pe.wait_ge(half_copied, 2 * m + half)
                by_dim = emb[parity][:, :].rearrange("p (i d) -> p d i", d=DIM)
                for i in range(HALF):
                    last = nc.tensor.transpose(target[0:PAIRS, i * 128:(i + 1) * 128],
                                               by_dim[:, half * HALF + i, :], ident[:, :])
                last.then_inc(half_transposed, 1)

            def contract(n, start, stop, z, between=None):
                columns = [slice(c * BANK, (c + 1) * BANK) for c in range(COLS // BANK)]

                def multiply(j, weights, part, first, last):
                    r = rows(*ORDER[j])
                    for c in columns:
                        for i, w in enumerate(weights):
                            mm = nc.tensor.matmul(z[:, c], w[0:r], part[0:r, c], start=first and i == 0,
                                                  stop=last and i == len(weights) - 1)
                    return mm

                def lo_part(j, tiles):
                    l, t = ORDER[j]
                    w = SPLIT_AT[l] + SPLITS[l].index(t)
                    if KIND[j] == "D":
                        pe.wait_ge(lo_ready_d, reached(n, j, "D"))
                    else:
                        pe.wait_ge(lo_ready_g, reached(n, j, "G"))
                    multiply(j, [whi[:, w, :]], lo[:, product_slot(j), :], False, False).then_inc(tile_used, tiles)

                assert KIND[stop - 1] == "F"
                late = None
                for j in range(start, stop):
                    l, t = ORDER[j]
                    if j == stop - 1 and late is not None:
                        lo_part(late, 1)
                        late = None
                    if KIND[j] == "F":
                        w = FULL_AT[l] + FULLS[l].index(t)
                        pe.wait_ge(product_ready, reached(n, j, "FDG"))
                        mm = multiply(j, [wfull[:, w, :]], prod[:, product_slot(j), :], j == start, j == stop - 1)
                        if late is None:
                            mm.then_inc(tile_used, 1)
                        else:
                            lo_part(late, 2)
                            late = None
                    else:
                        w = SPLIT_AT[l] + SPLITS[l].index(t)
                        pe.wait_ge(hi_ready, reached(n, j, "DG"))
                        multiply(j, [whi[:, w, :], wlo[:, w, :]], hi[:, part_slot(j), :], j == start, False)
                        if late is not None:
                            lo_part(late, 1)
                        late = j
                    if between and between[0] == j:
                        between[1]()

            pe.wait_ge(ident_ready, 1)
            transpose_half(0, 0, 0, xk[0], reuse=False)
            transpose_half(0, 0, 1, xk[1], reuse=False)
            pe.wait_ge(wlo_ready, 1)
            contract(PROLOGUE, L0, L2, accumulator(0, 1))
            transpose_half(1, 1, 0, xk[1])
            transpose_half(1, 1, 1, xk[1])
            pe.wait_ge(wlo_ready, 3)

            def step(n, parity):
                pe.wait_ge(z_evacuated[0], n + 1)
                contract(n, L1, L0, accumulator(1, parity))
                if not past_end(n, 2):
                    transpose_half(n + 2, parity, 0, xk[0])
                if not past_end(n, 1):
                    pe.wait_ge(z_evacuated[2], n + 1)
                    contract(n, L0, L2, accumulator(0, parity))
                pe.wait_ge(z_evacuated[1], n + 1)
                contract(n, L2, STEP, accumulator(2, parity), None if past_end(n, 2) else
                         (L2 + 1, lambda: transpose_half(n + 2, parity, 1, xk[0])))

            each_step(pe, step)

            pe.wait_ge(top_loaded, 9 * 16)
            halves = [slice(c * BANK, (c + 1) * BANK) for c in range(BATCH // BANK)]
            pe.wait_ge(z_evacuated[2], BLOCKS + 1)
            pe.wait_ge(direct01_summed, BLOCKS)
            for c, cols in enumerate(halves):
                if c == len(halves) - 1:
                    pe.wait_ge(direct2_summed, BLOCKS + 1)
                samples = slice(BLOCK + c * BANK, BLOCK + (c + 1) * BANK)
                for m in range(TOP1 // 128):
                    ms = slice(m * 128, (m + 1) * 128)
                    z = (acc + xk)[m][:, cols]
                    nc.tensor.matmul(z, wt1_sb[:, 0, ms], logit01[:, samples], start=True, stop=False)
                    nc.tensor.matmul(z, wt1_sb[:, 1, ms], logit2[:, samples], start=False, stop=False)
                    nc.tensor.matmul(z, wt1d_sb[:, ms], dense_sb[:, cols], start=False,
                                     stop=True).then_inc(top1_done, 1)
            for c, cols in enumerate(halves):
                for m in range(TOP2 // 128):
                    for k in range(TOP1 // 128):
                        pe.wait_ge(top1_ready, c * (TOP1 // 128) + max(k, m) + 1)
                        last = nc.tensor.matmul(acc[m][:, cols], wt2_sb[:, k, m * 128:(m + 1) * 128],
                                                top1[:, k, cols], start=(k == 0), stop=(k == TOP1 // 128 - 1))
                    last.then_inc(top2_done, 1)
            for c, cols in enumerate(halves):
                for k in range(TOP2 // 128):
                    pe.wait_ge(top2_ready, c * (TOP2 // 128) + k + 1)
                    last = nc.tensor.matmul(xk[0][0:1, cols], wt3_sb[:, k:k + 1], top2[:, k, cols],
                                            start=(k == 0), stop=(k == TOP2 // 128 - 1))
                last.then_inc(y_done, 1)


def kernel(**inputs):
    import numpy as np
    import concourse.bacc as bacc
    from concourse import mybir as mb
    from concourse.bass_utils import run_bass_kernel_spmd

    def a(name):
        return np.asarray(inputs[name])

    field = (np.arange(2)[:, None] * PAIRS + np.arange(PAIRS)[None, :]) % FIELDS
    ids = a("ids").reshape(BLOCKS, BLOCK, FIELDS)[:, :, field]
    ids = ids.transpose(2, 1, 0, 3).reshape(128, BLOCKS * PAIRS)
    start = np.cumsum([0] + [a(f"tbl_{f}").shape[0] for f in range(FIELDS - 1)]).astype(np.int32)
    base = np.broadcast_to(start[field][:, None, None, :], (2, BLOCK, BLOCKS, PAIRS)).reshape(128, BLOCKS * PAIRS)

    row = np.arange(ROWS0)[:, None]
    h = row % FIELDS
    k = (h + PER * np.array(SPLITS[0] + FULLS[0])[None, :] + row // FIELDS) % FIELDS
    w0 = a("L0_rec_w0")

    def by_tile(w, l):
        w = w.reshape(FIELDS * NEXT, LAYER)
        return np.concatenate([w[t * 128:(t + 1) * 128] for t in SPLITS[l] + FULLS[l]])

    w1 = a("L0_rec_w1")
    b1 = a("L0_rec_b1")
    arrays = {
        "ids": ids,
        "base": base,
        "table": np.concatenate([a(f"tbl_{f}") for f in range(FIELDS)]),
        "w0": w0[h, k],
        "w0t": w0[k, h],
        "w1": by_tile(np.concatenate([w1[:, :, NEXT:], w1[:, :, :NEXT]], axis=2), 1),
        "w2": by_tile(a("L0_rec_w2"), 2),
        "b0": a("L0_rec_b0").reshape(LAYER, 1),
        "b1": np.concatenate([b1[NEXT:], b1[:NEXT]]).reshape(LAYER, 1),
        "b2": a("L0_rec_b2").reshape(LAYER, 1),
        "dense": a("dense_ctx").T,
        "wt1": a("W_top1"),
        "bt1": a("b_top1").reshape(TOP1 // 128, 128).T,
        "wt2": a("W_top2"),
        "bt2": a("b_top2").reshape(TOP2 // 128, 128).T,
        "wt3": a("W_top3").reshape(TOP2 // 128, 128).T,
    }
    arrays = {n: np.ascontiguousarray(v) for n, v in arrays.items()}

    nc = bacc.Bacc("TRN2", target_bir_lowering=False, num_devices=1, dynamic_dma_scratch_size=4096)
    aps = [nc.dram_tensor(n, v.shape, mb.dt.from_np(v.dtype), kind="ExternalInput").ap() for n, v in arrays.items()]
    out = nc.dram_tensor("out", (BATCH, 1), mb.dt.float32, kind="ExternalOutput").ap()
    build(nc, *aps, out)
    r = run_bass_kernel_spmd(nc, [arrays], core_ids=[0])
    return r.results[0]["out"]
```

```python
import concourse.bass as bass
from concourse import mybir
from contextlib import ExitStack

BATCH, FIELDS, DIM = 1024, 39, 16
LAYER = 128
NEXT = LAYER // 2
BLOCK = 64
BLOCKS = BATCH // BLOCK
COLS = BLOCK * DIM
BANK = 512
PAIRS = (FIELDS + 1) // 2
SHIFTS = FIELDS // 2 + 1
PER = 3
T0 = -(-SHIFTS // PER)
T1 = -(-FIELDS * NEXT // 128)
ROWS0 = PER * FIELDS
LAST0 = (SHIFTS - PER * (T0 - 1)) * FIELDS
SROWS = FIELDS + PAIRS
COPIES = 8
STEP = 2 * T1 + T0
SHARE = 4
TOP1, TOP2 = 512, 256
TILES1, TILES2 = TOP1 // 128, TOP2 // 128
HALVES = BATCH // BANK
AT_ONCE = 128 // DIM
GROUPS = -(-PAIRS // AT_ONCE)

KINDS = ["GFDGDFF", "GFDGF" * 2 + "GFHGF" + "GFDGF", "GGDGF" + "GFDGF" + "GFHGF" + "GFDGF"]
SHORT = 12
assert all(k.count("H") == 1 and k[SHORT] == "H" for k in KINDS[1:])
SPLITS = [[t for t, k in enumerate(ks) if k != "F"] for ks in KINDS]
FULLS = [[t for t, k in enumerate(ks) if k == "F"] for ks in KINDS]
SPLIT_AT = [0, len(SPLITS[0]), len(SPLITS[0]) + len(SPLITS[1])]
FULL_AT = [0, len(FULLS[0]), len(FULLS[0]) + len(FULLS[1])]
N_SPLIT = sum(map(len, SPLITS))
N_FULL = sum(map(len, FULLS))
PRODS, PARTS = 6, 4

ORDER = [(1, t) for t in range(T1)] + [(0, t) for t in range(T0)] + [(2, t) for t in range(T1)]
L1, L0, L2 = 0, T1, T1 + T0
KIND = [KINDS[l][t] for l, t in ORDER]


def rows(l, t):
    if l == 0:
        return ROWS0 if t < T0 - 1 else LAST0
    return 128


def first_field(t):
    return 2 * t - (t > SHORT)


PROLOGUE = -1
LAST = BLOCKS - 1


def is_step(n, m):
    return isinstance(n, int) and n == m


def executed(n):
    js = range(L0, L2) if is_step(n, PROLOGUE) else range(STEP)
    return [j for j in js if not (is_step(n, LAST) and L0 <= j < L2)]


def reached(n, j, kinds):
    of_step = sum(k in kinds for k in KIND)
    if is_step(n, PROLOGUE):
        return sum(KIND[i] in kinds for i in range(L0, j + 1))
    prologue = sum(k in kinds for k in KINDS[0])
    if j < 0:
        return n * of_step + prologue - sum(k in kinds for k in KIND[STEP + j + 1:])
    return n * of_step + prologue + sum(KIND[i] in kinds for i in executed(n) if i <= j)


def earlier(n, j):
    return [i for i in reversed(executed(n)) if i < j] + list(range(-1, -STEP - 1, -1))


def product_slot(j):
    return j % PRODS


def product_before(n, j):
    return next(i for i in earlier(n, j) if product_slot(i % STEP) == product_slot(j))


def part_slot(j):
    return sum(k != "F" for k in KIND[:j]) % PARTS


def parts_before(n, j):
    return next(i for i in earlier(n, j) if KIND[i] != "F" and part_slot(i % STEP) == part_slot(j))


def build(nc, ids, base, table, w0, w0t, w1, w2, b0, b1, b2, dense, wt1, bt1, wt2, bt2, wt3, out):
    f32, f32r, i32 = mybir.dt.float32, mybir.dt.float32r, mybir.dt.int32
    ALU = mybir.AluOpType
    ACT = mybir.ActivationFunctionType
    AX = mybir.AxisListType

    x0_rows = nc.dram_tensor("x0_rows", [BLOCKS, SROWS, COLS], f32, kind="Internal").ap()
    x0_replicas = nc.dram_tensor("x0_replicas", [BLOCKS, FIELDS, COPIES, COLS], f32, kind="Internal").ap()

    with ExitStack() as ctx:
        def sb(name, shape, dt=f32):
            return ctx.enter_context(nc.sbuf_tensor(name, shape, dt))

        def ps(name):
            return ctx.enter_context(nc.psum_tensor(name, [128, COLS], f32))

        def sem(name):
            return ctx.enter_context(nc.semaphore(name))

        rows_idx = sb("rows_idx", [128, BLOCKS * PAIRS], i32)
        base_sb = sb("base_sb", [128, BLOCKS * PAIRS], i32)
        block_idx = [sb(f"block_idx{p}", [128, PAIRS], i32) for p in range(2)]
        emb = [sb(f"emb{p}", [128, PAIRS * DIM]) for p in range(2)]
        ident = sb("ident", [128, 128])
        x0T = sb("x0T", [128, GROUPS, 128])
        stack_at = nc.sbuf_base
        x0_stack = sb("x0_stack", [128, COLS])
        x0_rot = sb("x0_rot", [128, T0, COLS])
        spread_at = nc.sbuf_base
        spread = sb("spread", [128, T1, COLS])
        prod_at = nc.sbuf_base
        prod = sb("prod", [128, PRODS, COLS])
        lo = nc.alloc_sbuf_tensor_at("lo", [128, PRODS, COLS], f32r, offset=prod_at)
        hi = sb("hi", [128, PARTS, COLS], f32r)
        direct01 = sb("direct01", [128, COLS])
        direct2 = sb("direct2", [128, COLS])
        logit01 = sb("logit01", [128, BLOCK + BATCH])
        logit2 = sb("logit2", [128, BLOCK + BATCH])
        wfull = sb("wfull", [128, N_FULL, LAYER])
        whi = sb("whi", [128, N_SPLIT, LAYER], f32r)
        wlo = sb("wlo", [128, N_SPLIT, LAYER], f32r)
        bias = sb("bias", [LAYER, 3])
        wt3_sb = sb("wt3_sb", [128, TOP2 // 128])
        bt1_sb = sb("bt1_sb", [128, TOP1 // 128])
        bt2_sb = sb("bt2_sb", [128, TOP2 // 128])
        acc = [ps("acc0"), ps("acc1")]
        xk = [ps("xk0"), ps("xk1")]

        STAGED = -(-(N_SPLIT + len(FULLS[0]) + T0) * LAYER // COLS)
        stage = spread[:, T1 - STAGED:T1, :].rearrange("p t c -> p (t c)").rearrange("p (w s) -> p w s", s=LAYER)
        w_stage = stage[:, 0:N_SPLIT, :]
        w0f_stage = stage[:, N_SPLIT:N_SPLIT + len(FULLS[0]), :]
        w0t_stage = stage[:, N_SPLIT + len(FULLS[0]):N_SPLIT + len(FULLS[0]) + T0, :]
        pairs_r = nc.alloc_sbuf_tensor_at("pairs_r", [128, 1 + T0, COLS], f32r, offset=stack_at)
        spread_r = nc.alloc_sbuf_tensor_at("spread_r", [128, T1, COLS], f32r, offset=spread_at)
        wt1_sb = x0_rot[:, 0, :].rearrange("p (t n) -> p t n", n=TOP1)
        wt2_sb = x0_rot[:, 1, :].rearrange("p (t n) -> p t n", n=TOP2)
        dense_sb = x0_rot[0:DIM, 2, 0:BATCH]
        wt1d_sb = x0_rot[0:DIM, 3, 0:TOP1]
        wt1_hi, wt1_lo = (pairs_r[:, p, :].rearrange("p (t n) -> p t n", n=TOP1) for p in (5, 6))
        wt2_hi, wt2_lo = (pairs_r[:, p, :].rearrange("p (t n) -> p t n", n=TOP2) for p in (7, 0))
        logits_r = [pairs_r[:, 1:3, :], spread_r[:, 18:20, :]]
        top1, top1_hi, top1_lo = ([place[:, 6 * c + p:6 * c + p + 2, :].rearrange("p t (m s) -> p (t m) s", s=BANK)
                                   for c in range(HALVES)]
                                  for place, p in ((spread, 0), (spread_r, 2), (spread_r, 4)))
        top2 = spread[:, 12:12 + TILES2, :]
        y_sb = spread[0:1, 14, :]

        ids_loaded = sem("ids_loaded")
        idx_added = sem("idx_added")
        idx_ready = sem("idx_ready")
        rows_gathered = [sem(f"rows_gathered{p}") for p in range(2)]
        ident_zero = sem("ident_zero")
        ident_ready = sem("ident_ready")
        rows_transposed = sem("rows_transposed")
        rows_copied = sem("rows_copied")
        rows_written = sem("rows_written")
        replicas_written = sem("replicas_written")
        pairs_loaded = [sem(f"pairs_loaded{t}") for t in range(T0)]
        spread_loaded = [sem(f"spread_loaded{q}") for q in range(T1 // SHARE)]
        w0_loaded = sem("w0_loaded")
        w0_cleared = sem("w0_cleared")
        w0_summed = sem("w0_summed")
        w12_loaded = sem("w12_loaded")
        whi_ready = sem("whi_ready")
        wlo_ready = sem("wlo_ready")
        top_loaded = sem("top_loaded")
        bias_loaded = sem("bias_loaded")
        product_ready = sem("product_ready")
        hi_ready = sem("hi_ready")
        lo_ready_d = sem("lo_ready_d")
        lo_ready_g = sem("lo_ready_g")
        tile_used = sem("tile_used")
        xk_ready = [sem(f"xk{p}_ready") for p in range(2)]
        z_evacuated = [sem(f"z{l}_evacuated") for l in range(3)]
        direct2_cleared = sem("direct2_cleared")
        direct01_summed = sem("direct01_summed")
        direct2_summed = sem("direct2_summed")
        top_rounded = sem("top_rounded")
        top_split = sem("top_split")
        logits_rounded = sem("logits_rounded")
        logits_split = [sem(f"logits{c}_split") for c in range(HALVES)]
        top1_done = sem("top1_done")
        top1_rounded = sem("top1_rounded")
        top1_split = [sem(f"top1{c}_split") for c in range(HALVES)]
        top2_done = sem("top2_done")
        top2_ready = sem("top2_ready")
        y_done = sem("y_done")
        y_ready = sem("y_ready")
        y_stored = sem("y_stored")

        block = ctx.enter_context(nc.Block())

        def each_step(eng, step):
            with eng.Fori(0, BLOCKS // 2 - 1) as g:
                step(2 * g, 0)
                step(2 * g + 1, 1)
            step(LAST - 1, 0)
            step(LAST, 1)

        def top_bank(layer, c, m):
            bank = lambda z, i: z[:, i * BANK:(i + 1) * BANK]
            free, busy = accumulator(0, LAST % 2), accumulator(1, LAST % 2)
            if layer == 3:
                return bank(busy, c)
            places = ((free, xk[0]), (busy, xk[1])) if layer == 1 else ((free,), (xk[0],))
            return bank(places[c][m // 2], m % 2)

        def past_end(n, ahead):
            return isinstance(n, int) and n + ahead > LAST

        def accumulator(l, parity):
            return acc[1 - parity if l == 0 else parity]

        @block.sync
        def _(sp):
            def load_weights():
                n = len(SPLITS[0])
                sp.dma_start(w_stage[0:ROWS0, 0:n, :], w0[:, 0:n, :]).then_inc(w0_loaded, 16)
                sp.dma_start(w0f_stage[0:ROWS0, 0:len(FULLS[0]) - 1, :], w0[:, n:T0 - 1, :]).then_inc(w0_loaded, 16)
                sp.dma_start(w0f_stage[0:LAST0, len(FULLS[0]) - 1, :], w0[0:LAST0, T0 - 1, :]).then_inc(w0_loaded, 16)
                sp.dma_start(w0t_stage[0:ROWS0, 1:T0 - 1, :], w0t[:, 1:T0 - 1, :]).then_inc(w0_loaded, 16)
                sp.dma_start(w0t_stage[0:LAST0, T0 - 1, :], w0t[0:LAST0, T0 - 1, :]).then_inc(w0_loaded, 16)
                sp.wait_ge(w0_cleared, 1)
                sp.dma_start(w0t_stage[FIELDS:ROWS0, 0, :], w0t[FIELDS:ROWS0, 0, :]).then_inc(w0_loaded, 16)
                for l, b in enumerate((b0, b1, b2)):
                    sp.dma_start(bias[:, l:l + 1], b).then_inc(bias_loaded, 16)
                for l, w in ((1, w1), (2, w2)):
                    n, f = len(SPLITS[l]), len(FULLS[l])
                    sp.dma_start(w_stage[:, SPLIT_AT[l]:SPLIT_AT[l] + n, :],
                                 w[0:n * 128, :].rearrange("(t p) s -> p t s", p=128)).then_inc(w12_loaded, 16)
                    sp.dma_start(wfull[:, FULL_AT[l]:FULL_AT[l] + f, :],
                                 w[n * 128:, :].rearrange("(t p) s -> p t s", p=128)
                                 ).then_inc(w12_loaded, 16)

            def load_top():
                sp.dma_start(wt1_sb[0:NEXT, 0, :], wt1[NEXT:2 * NEXT, :]).then_inc(top_loaded, 16)
                sp.dma_start(wt1_sb[NEXT:128, 0, :], wt1[0:NEXT, :]).then_inc(top_loaded, 16)
                sp.dma_start(wt1_sb[:, 1, :], wt1[128:256, :]).then_inc(top_loaded, 16)
                sp.dma_start(wt1d_sb, wt1[256:256 + DIM, :]).then_inc(top_loaded, 16)
                sp.dma_start(wt2_sb, wt2.rearrange("(t p) n -> p t n", p=128)).then_inc(top_loaded, 16)
                sp.dma_start(wt3_sb[:, :], wt3).then_inc(top_loaded, 16)
                sp.dma_start(bt1_sb[:, :], bt1).then_inc(top_loaded, 16)
                sp.dma_start(bt2_sb[:, :], bt2).then_inc(top_loaded, 16)
                sp.dma_start(dense_sb, dense).then_inc(top_loaded, 16)

            def rows_ap(m, row, dims):
                return bass.AP(x0_rows.tensor, (m * SROWS + row) * COLS, dims)

            def write_rows(m):
                sp.wait_ge(rows_copied, m + 1)
                sp.nop(nofuse=True)
                for g in range(GROUPS):
                    first = g * AT_ONCE
                    fields = min(AT_ONCE, PAIRS - first)
                    sp.dma_start(rows_ap(m, first, [[BLOCK, fields * DIM], [FIELDS * COLS, 2], [1, BLOCK]]),
                                 x0T[0:fields * DIM, g:g + 1, 0:BLOCK].to_broadcast([fields * DIM, 2, BLOCK])
                                 ).then_inc(rows_written, 16)
                    fields = min(AT_ONCE, FIELDS - PAIRS - first)
                    sp.dma_start(rows_ap(m, PAIRS + first, [[BLOCK, fields * DIM], [1, BLOCK]]),
                                 x0T[0:fields * DIM, g, BLOCK:]).then_inc(rows_written, 16)

            def write_replicas(m):
                sp.wait_ge(rows_written, 6 * 16 * (m + 1))
                if not isinstance(m, int):
                    sp.nop(nofuse=True)
                sp.dma_start(bass.AP(x0_replicas.tensor, m * (FIELDS * COPIES * COLS),
                                     [[COPIES * COLS, FIELDS], [COLS, COPIES], [1, COLS]]),
                             bass.AP(x0_rows.tensor, m * (SROWS * COLS),
                                     [[COLS, FIELDS], [0, COPIES], [1, COLS]])).then_inc(replicas_written, 16)

            def load_pairs(m):
                sp.wait_ge(rows_written, 6 * 16 * (m + 1))
                sp.nop(nofuse=True)
                sp.dma_start(x0_stack[0:ROWS0, :], rows_ap(m, 0, [[0, PER], [COLS, FIELDS], [1, COLS]])
                             ).then_inc(pairs_loaded[0], 16)
                for t in range(T0):
                    r = rows(0, t)
                    sp.dma_start(x0_rot[0:r, t, :],
                                 rows_ap(m, PER * t, [[COLS, r // FIELDS], [COLS, FIELDS], [1, COLS]])
                                 ).then_inc(pairs_loaded[t], 16)

            def load_spread(m, t):
                n = COPIES * (1 if t == SHORT else 2)
                sp.dma_start(spread[:, t, :],
                             bass.AP(x0_replicas.tensor, (m * FIELDS + first_field(t)) * (COPIES * COLS),
                                     [[COLS, n], [0, 128 // n], [1, COLS]])
                             ).then_inc(spread_loaded[t // SHARE], 16)

            sp.dma_start(rows_idx[:, :], ids).then_inc(ids_loaded, 16)
            sp.dma_start(base_sb[:, :], base).then_inc(ids_loaded, 16)
            load_weights()
            write_rows(0)
            load_pairs(0)
            write_replicas(0)
            sp.wait_ge(replicas_written, 16)
            for t in range(T1):
                if t == T1 - STAGED:
                    sp.wait_ge(wlo_ready, 3)
                load_spread(0, t)
            write_rows(1)
            sp.wait_ge(product_ready, T0)
            load_pairs(1)
            write_replicas(1)

            def step(n, parity):
                if not past_end(n, 2):
                    write_rows(n + 2)
                if not past_end(n, 1):
                    sp.wait_ge(replicas_written, 16 * n + 32)
                    sp.nop(nofuse=True)
                    for t in range(T1):
                        sp.wait_ge(product_ready, reached(n, L2 + t, "FDGH"))
                        load_spread(n + 1, t)
                if not past_end(n, 2):
                    load_pairs(n + 2)
                    write_replicas(n + 2)
                elif not past_end(n, 1):
                    load_top()

            each_step(sp, step)
            sp.wait_ge(y_ready, 2)
            sp.dma_start(out.rearrange("b o -> o b"), y_sb).then_inc(y_stored, 16)
            sp.wait_ge(y_stored, 16)

        @block.gpsimd
        def _(pool):
            def take_indices(m, parity, reuse=True):
                if reuse:
                    pool.wait_ge(rows_gathered[parity], 8 * PAIRS * (m - parity))
                pool.nop(nofuse=True)
                nc.gpsimd.tensor_copy(block_idx[parity][:, :], rows_idx[:, bass.ds(m * PAIRS, PAIRS)]
                                      ).then_inc(idx_ready, 1)
                pool.wait_ge(idx_ready, m + 1)
                if reuse:
                    pool.wait_ge(rows_transposed, m - 1)
                pool.nop(nofuse=True)

            def gather(parity, start, stop):
                for i in range(start, stop):
                    pool.indirect_dma_start(
                        out=emb[parity][:, i * DIM:(i + 1) * DIM], out_offset=None, in_=table,
                        in_offset=bass.IndirectOffsetOnAxis(ap=block_idx[parity][:, i:i + 1], axis=0),
                    ).then_inc(rows_gathered[parity], 16)

            def subtract(n, j):
                r = rows(*ORDER[j])
                pool.wait_ge(hi_ready, reached(n, j, "DGH"))
                nc.gpsimd.tensor_tensor(lo[0:r, product_slot(j), :], prod[0:r, product_slot(j), :],
                                        hi[0:r, part_slot(j), :].bitcast(f32), ALU.subtract).then_inc(lo_ready_g, 1)

            nc.gpsimd.memset(ident[:, :], 0.0).then_inc(ident_zero, 1)
            pool.wait_ge(ids_loaded, 32)
            nc.gpsimd.tensor_tensor(rows_idx[:, :], rows_idx[:, :], base_sb[:, :], ALU.add).then_inc(idx_added, 1)
            pool.wait_ge(idx_added, 1)
            take_indices(0, 0, reuse=False)
            gather(0, 0, PAIRS)
            pool.wait_ge(ident_zero, 1)
            nc.gpsimd.affine_select(out=ident[:, :], in_=ident[:, :], compare_op=ALU.not_equal, fill=1.0, base=0,
                                    pattern=[[-1, 128]], channel_multiplier=1).then_inc(ident_ready, 1)
            take_indices(1, 1, reuse=False)
            gather(1, 0, 14)

            def split_top(i):
                w, w_hi, w_lo = ((wt1_sb, wt1_hi, wt1_lo), (wt2_sb, wt2_hi, wt2_lo))[i]
                pool.wait_ge(top_rounded, i + 1)
                nc.gpsimd.tensor_tensor(w_lo, w, w_hi.bitcast(f32), ALU.subtract).then_inc(top_split, 1)

            def split_logits():
                for i, logit in enumerate((logit01, logit2)):
                    pool.wait_ge(logits_rounded, i + 1)
                    nc.gpsimd.tensor_tensor(logits_r[0][:, i, BANK:], logit[:, BLOCK:BLOCK + BANK],
                                            logits_r[0][:, i, 0:BANK].bitcast(f32), ALU.subtract
                                            ).then_inc(logits_split[0], 1)

            def split_top1(m):
                pool.wait_ge(top1_rounded, m + 1)
                nc.gpsimd.tensor_tensor(top1_lo[0][:, m, :], top1[0][:, m, :], top1_hi[0][:, m, :].bitcast(f32),
                                        ALU.subtract).then_inc(top1_split[0], 1)

            def layer(n, l, m=None, parity=0, gathers=(0, 0)):
                at, tiles = (L0, L1, L2)[l], [t for t, k in enumerate(KINDS[l]) if k == "G"]
                start, stop = gathers
                if past_end(n, 1):
                    after = {1: {3: lambda: split_top(0), 8: lambda: split_top(1), 15: split_logits},
                             2: {8: lambda: split_top1(0), 10: lambda: split_top1(1), 13: lambda: split_top1(2),
                                 15: lambda: split_top1(3)}}[l]
                else:
                    after = {}
                between = max(1, len(tiles) - (2 if l == 1 else 0))
                for i, t in enumerate(tiles):
                    subtract(n, at + t)
                    if t in after:
                        after[t]()
                    if m is not None and i < between:
                        gather(parity, start + i * (stop - start) // between,
                               start + (i + 1) * (stop - start) // between)

            GATHERS = {0: (0, 4), 2: (4, 12), 1: (12, PAIRS)}
            layer(PROLOGUE, 0, 1, 1, (14, PAIRS))
            take_indices(2, 0)
            gather(0, 0, 8)
            layer(0, 1, 2, 0, (8, PAIRS))

            def step(n, parity):
                m = None if past_end(n, 3) else n + 3
                if m is not None:
                    take_indices(m, 1 - parity)
                if not past_end(n, 1):
                    layer(n, 0, m, 1 - parity, GATHERS[0])
                layer(n, 2, m, 1 - parity, GATHERS[2])
                if not past_end(n, 1):
                    layer(n + 1, 1, m, 1 - parity, GATHERS[1])

            with pool.Fori(0, (BLOCKS - 3) // 2) as g:
                step(2 * g, 0)
                step(2 * g + 1, 1)
            for n in range((BLOCKS - 3) // 2 * 2, BLOCKS):
                step(n, n % 2)

        @block.scalar
        def _(act):
            def copy_rows(m, source, reuse=True):
                act.wait_ge(rows_transposed, m + 1)
                if reuse:
                    act.wait_ge(rows_written, 6 * 16 * m)
                whole, rest = GROUPS - 1, (PAIRS - (GROUPS - 1) * AT_ONCE) * DIM
                nc.scalar.activation(x0T[:, 0:whole, :], source[:, 0:whole * 128], ACT.Copy)
                nc.scalar.activation(x0T[0:rest, whole, :], source[0:rest, whole * 128:GROUPS * 128],
                                     ACT.Copy).then_inc(rows_copied, 1)

            def relu(dst, src, l, first, last):
                return nc.scalar.activation(dst, src, ACT.Relu, bias=bias[first:last, l:l + 1])

            def evacuate(l, m, z, done, copied=None, reuse=True):
                if copied is not None:
                    act.wait_ge(rows_copied, copied)
                act.wait_ge(tile_used, done)
                if l == 0:
                    relu(xk[0][0:NEXT, :], z[0:NEXT, :], 0, 0, NEXT)
                    relu(xk[0][NEXT:128, :], z[0:NEXT, :], 0, 0, NEXT).then_inc(xk_ready[0], 1)
                    if reuse:
                        act.wait_ge(direct01_summed, m)
                    last = relu(direct01[NEXT:128, :], z[NEXT:128, :], 0, NEXT, 128)
                elif l == 1:
                    relu(xk[1][0:NEXT, :], z[NEXT:128, :], 1, NEXT, 128)
                    relu(xk[1][NEXT:128, :], z[NEXT:128, :], 1, NEXT, 128).then_inc(xk_ready[1], 1)
                    return
                else:
                    act.wait_ge(direct2_summed, m + 1)
                    last = relu(direct2[:, :], z[:, :], 2, 0, 128)
                last.then_inc(z_evacuated[l], 1)

            def evacuate_direct1(z):
                relu(direct01[0:NEXT, :], z[0:NEXT, :], 1, 0, NEXT).then_inc(z_evacuated[1], 1)

            def round_hi(n, start, stop):
                for j in range(start, stop):
                    if KIND[j] != "F":
                        r = rows(*ORDER[j])
                        act.wait_ge(product_ready, reached(n, j, "FDGH"))
                        if not is_step(n, PROLOGUE) or SPLITS[0].index(ORDER[j][1]) >= PARTS:
                            act.wait_ge(tile_used, reached(n, parts_before(n, j), "FDGH"))
                        nc.scalar.activation(hi[0:r, part_slot(j), :], prod[0:r, product_slot(j), :],
                                             ACT.Copy).then_inc(hi_ready, 1)

            def round_top():
                act.wait_ge(top_loaded, 9 * 16)
                nc.scalar.activation(wt1_hi, wt1_sb, ACT.Copy).then_inc(top_rounded, 1)
                nc.scalar.activation(wt2_hi, wt2_sb, ACT.Copy).then_inc(top_rounded, 1)

            def round_logits(c):
                if c == 0:
                    act.wait_ge(top_split, 2)
                samples = slice(BLOCK + c * BANK, BLOCK + (c + 1) * BANK)
                act.wait_ge(direct01_summed, (c + 1) * BANK // BLOCK)
                nc.scalar.activation(logits_r[c][:, 0, 0:BANK], logit01[:, samples], ACT.Copy
                                     ).then_inc(logits_rounded, 1)
                act.wait_ge(direct2_summed, (c + 1) * BANK // BLOCK + 1)
                nc.scalar.activation(logits_r[c][:, 1, 0:BANK], logit2[:, samples], ACT.Copy
                                     ).then_inc(logits_rounded, 1)

            def relu_top1(c, start, stop):
                for m in range(start, stop):
                    act.wait_ge(top1_done, c * TILES1 + m + 1)
                    z = top_bank(1, c, m)
                    nc.scalar.activation(top1[c][:, m, :], z, ACT.Relu, bias=bt1_sb[:, m:m + 1])
                    nc.scalar.activation(top1_hi[c][:, m, :], z, ACT.Relu, bias=bt1_sb[:, m:m + 1]
                                         ).then_inc(top1_rounded, 1)

            def relu_top2(c):
                for m in range(TILES2):
                    act.wait_ge(top2_done, c * TILES2 + m + 1)
                    nc.scalar.activation(top2[:, m, c * BANK:(c + 1) * BANK], top_bank(2, c, m), ACT.Relu,
                                         bias=bt2_sb[:, m:m + 1]).then_inc(top2_ready, 1)

            def copy_y(c):
                act.wait_ge(y_done, c + 1)
                nc.scalar.activation(y_sb[:, c * BANK:(c + 1) * BANK], top_bank(3, c, 0)[0:1, :], ACT.Copy
                                     ).then_inc(y_ready, 1)

            act.sem_inc(z_evacuated[2], 1)
            for l in range(3):
                act.wait_ge((w0_summed, w12_loaded, w12_loaded)[l], (1, 64, 64)[l])
                n, r = len(SPLITS[l]), rows(l, 0)
                nc.scalar.activation(whi[0:r, SPLIT_AT[l]:SPLIT_AT[l] + n, :],
                                     w_stage[0:r, SPLIT_AT[l]:SPLIT_AT[l] + n, :], ACT.Copy).then_inc(whi_ready, 1)
            act.wait_ge(bias_loaded, 48)
            copy_rows(0, xk[0], reuse=False)
            round_hi(PROLOGUE, L0, L2)
            evacuate(0, 0, accumulator(0, 1), T0, copied=1, reuse=False)
            copy_rows(1, xk[1])
            XK1_AFTER, DIRECT1_AFTER, COPY_AFTER = 3, 4, 5
            Z0_AFTER, Z2_AFTER = 5, 4
            TOP_AFTER, TOP1_AFTER = (4, 13), 8
            round_hi(0, L1, L1 + Z2_AFTER)

            def step(n, parity):
                z1, z0, z2 = (accumulator(l, parity) for l in (1, 0, 2))
                if past_end(n, 1):
                    round_hi(n, L1 + Z2_AFTER, L1 + TOP_AFTER[0])
                    round_top()
                    round_hi(n, L1 + TOP_AFTER[0], L1 + TOP_AFTER[1])
                    round_logits(0)
                    round_hi(n, L1 + TOP_AFTER[1], L0)
                    evacuate(1, n, z1, reached(n, L0 - 1, "FDGH"))
                    evacuate_direct1(z1)
                    round_hi(n, L2, L2 + TOP1_AFTER)
                    for m in range(TILES1):
                        relu_top1(0, m, m + 1)
                        round_hi(n, L2 + TOP1_AFTER + 2 * m, L2 + TOP1_AFTER + 2 * m + 2)
                    round_hi(n, L2 + TOP1_AFTER + 2 * TILES1, STEP)
                    evacuate(2, n, z2, reached(n, STEP - 1, "FDGH"))
                    return
                round_hi(n, L1 + Z2_AFTER, L0 + XK1_AFTER)
                evacuate(1, n, z1, reached(n, L0 - 1, "FDGH"), copied=2)
                round_hi(n, L0 + XK1_AFTER, L0 + DIRECT1_AFTER)
                evacuate_direct1(z1)
                round_hi(n, L0 + DIRECT1_AFTER, L0 + COPY_AFTER)
                if not past_end(n, 2):
                    copy_rows(n + 2, xk[0])
                round_hi(n, L0 + COPY_AFTER, L2 + Z0_AFTER)
                evacuate(0, n + 1, z0, reached(n, L2 - 1, "FDGH"), copied=None if past_end(n, 2) else n + 3)
                round_hi(n, L2 + Z0_AFTER, STEP)
                round_hi(n + 1, L1, L1 + Z2_AFTER)
                evacuate(2, n, z2, reached(n, STEP - 1, "FDGH"))

            each_step(act, step)
            round_logits(1)
            relu_top2(0)
            relu_top1(1, 0, TILES1)
            copy_y(0)
            relu_top2(1)
            copy_y(1)

        @block.vector
        def _(dve):
            nc.vector.memset(w0t_stage[:, 0, :], 0.0).then_inc(w0_cleared, 1)
            nc.vector.memset(direct2[:, :], 0.0).then_inc(direct2_cleared, 1)
            dve.wait_ge(direct2_cleared, 1)
            dve.wait_ge(w0_loaded, 6 * 16)
            n, f = len(SPLITS[0]), len(FULLS[0])
            nc.vector.tensor_tensor(wfull[0:ROWS0, 0:f - 1, :], w0f_stage[0:ROWS0, 0:f - 1, :],
                                    w0t_stage[0:ROWS0, n:T0 - 1, :], ALU.add)
            nc.vector.tensor_tensor(wfull[0:LAST0, f - 1, :], w0f_stage[0:LAST0, f - 1, :],
                                    w0t_stage[0:LAST0, T0 - 1, :], ALU.add)
            nc.vector.tensor_tensor(w_stage[0:ROWS0, 0:n, :], w_stage[0:ROWS0, 0:n, :],
                                    w0t_stage[0:ROWS0, 0:n, :], ALU.add).then_inc(w0_summed, 1)
            dve.wait_ge(w0_summed, 1)
            for l in range(3):
                dve.wait_ge(whi_ready, l + 1)
                part = slice(SPLIT_AT[l], SPLIT_AT[l] + len(SPLITS[l]))
                r = rows(l, 0)
                nc.vector.tensor_tensor(wlo[0:r, part, :], w_stage[0:r, part, :], whi[0:r, part, :].bitcast(f32),
                                        ALU.subtract).then_inc(wlo_ready, 1)

            def product(n, j):
                l, t = ORDER[j]
                r = rows(l, t)
                if not is_step(n, PROLOGUE) or j - L0 >= PRODS:
                    dve.wait_ge(tile_used, reached(n, product_before(n, j), "FDGH"))
                in0, in1 = (x0_stack[0:r, :], x0_rot[0:r, t, :]) if l == 0 else (spread[0:r, t, :], xk[l - 1][0:r, :])
                nc.vector.tensor_tensor(prod[0:r, product_slot(j), :], in0, in1, ALU.mult).then_inc(product_ready, 1)

            def subtract(n, j):
                r = rows(*ORDER[j])
                dve.wait_ge(hi_ready, reached(n, j, "DGH"))
                if KIND[j] == "H":
                    half = hi[NEXT:128, part_slot(j), :]
                    nc.vector.tensor_tensor(half, prod[NEXT:128, product_slot(j), :], half.bitcast(f32),
                                            ALU.subtract).then_inc(lo_ready_d, 1)
                    return
                nc.vector.tensor_tensor(lo[0:r, product_slot(j), :], prod[0:r, product_slot(j), :],
                                        hi[0:r, part_slot(j), :].bitcast(f32), ALU.subtract).then_inc(lo_ready_d, 1)

            DELAY = 2

            def tiles(n, start, stop):
                for j in range(start, stop):
                    l, t = ORDER[j]
                    if l == 0:
                        dve.wait_ge(pairs_loaded[t], (32 if t == 0 else 16) * (n + 2))
                    if l > 0 and t == 0:
                        dve.wait_ge(xk_ready[l - 1], n + 1)
                    if l == 1 and t % SHARE == 0:
                        dve.wait_ge(spread_loaded[t // SHARE], SHARE * 16 * (n + 1))
                    product(n, j)
                    if j - DELAY >= start and KIND[j - DELAY] in "DH":
                        subtract(n, j - DELAY)
                    if l == 1 and t == T1 // 2:
                        sum_direct2(n)
                    if l == 2 and t == 3:
                        dve.wait_ge(z_evacuated[1], n + 1)
                        sum_direct01(n)
                for j in range(stop - DELAY, stop):
                    if KIND[j] in "DH":
                        subtract(n, j)

            def sum_over_d(dst, src, column):
                return nc.vector.tensor_reduce(dst[:, bass.ds(column, BLOCK)],
                                               src[:, :].rearrange("p (d s) -> p s d", d=DIM), AX.X, ALU.add)

            def sum_direct01(m):
                sum_over_d(logit01, direct01, BLOCK * m + BLOCK).then_inc(direct01_summed, 1)

            def sum_direct2(n):
                dve.wait_ge(z_evacuated[2], n + 1)
                sum_over_d(logit2, direct2, BLOCK * n).then_inc(direct2_summed, 1)

            tiles(PROLOGUE, L0, L2)

            def step(n, parity):
                if past_end(n, 1):
                    tiles(n, L1, L0)
                    tiles(n, L2, STEP)
                else:
                    tiles(n, L1, STEP)

            each_step(dve, step)
            sum_direct2(BLOCKS)
            for i, logit in enumerate((logit01, logit2)):
                dve.wait_ge(logits_rounded, 2 + i + 1)
                nc.vector.tensor_tensor(logits_r[1][:, i, BANK:], logit[:, BLOCK + BANK:BLOCK + BATCH],
                                        logits_r[1][:, i, 0:BANK].bitcast(f32), ALU.subtract
                                        ).then_inc(logits_split[1], 1)
            for m in range(TILES1):
                dve.wait_ge(top1_rounded, TILES1 + m + 1)
                nc.vector.tensor_tensor(top1_lo[1][:, m, :], top1[1][:, m, :], top1_hi[1][:, m, :].bitcast(f32),
                                        ALU.subtract).then_inc(top1_split[1], 1)

        @block.tensor
        def _(pe):
            def transpose_rows(m, parity, target):
                pe.wait_ge(rows_gathered[parity], 8 * PAIRS * (m + 2 - parity))
                pe.nop(nofuse=True)
                for g in range(GROUPS):
                    width = min(128, PAIRS * DIM - g * 128)
                    last = nc.tensor.transpose(target[0:width, g * 128:(g + 1) * 128],
                                               emb[parity][:, g * 128:g * 128 + width], ident[:, :])
                last.then_inc(rows_transposed, 1)

            def contract(n, start, stop, z, between=None):
                columns = [slice(c * BANK, (c + 1) * BANK) for c in range(COLS // BANK)]

                def multiply(j, weights, part, first, last, r=None):
                    r = r or rows(*ORDER[j])
                    for c in columns:
                        for i, w in enumerate(weights):
                            mm = nc.tensor.matmul(z[:, c], w[0:r], part[0:r, c], start=first and i == 0,
                                                  stop=last and i == len(weights) - 1)
                    return mm

                def lo_part(j, tiles):
                    l, t = ORDER[j]
                    w = SPLIT_AT[l] + SPLITS[l].index(t)
                    part = hi[:, part_slot(j), :] if KIND[j] == "H" else lo[:, product_slot(j), :]
                    if KIND[j] in "DH":
                        pe.wait_ge(lo_ready_d, reached(n, j, "DH"))
                    else:
                        pe.wait_ge(lo_ready_g, reached(n, j, "G"))
                    multiply(j, [whi[:, w, :]], part, False, False).then_inc(tile_used, tiles)

                assert KIND[stop - 1] == "F"
                late = None
                for j in range(start, stop):
                    l, t = ORDER[j]
                    if j == stop - 1 and late is not None:
                        lo_part(late, 1)
                        late = None
                    if KIND[j] == "F":
                        w = FULL_AT[l] + FULLS[l].index(t)
                        pe.wait_ge(product_ready, reached(n, j, "FDGH"))
                        mm = multiply(j, [wfull[:, w, :]], prod[:, product_slot(j), :], j == start, j == stop - 1)
                        if late is None:
                            mm.then_inc(tile_used, 1)
                        else:
                            lo_part(late, 2)
                            late = None
                    else:
                        w = SPLIT_AT[l] + SPLITS[l].index(t)
                        pe.wait_ge(hi_ready, reached(n, j, "DGH"))
                        if KIND[j] == "H":
                            multiply(j, [wlo[:, w, :]], hi[:, part_slot(j), :], False, False, r=NEXT)
                        else:
                            multiply(j, [whi[:, w, :], wlo[:, w, :]], hi[:, part_slot(j), :], j == start, False)
                        if late is not None:
                            lo_part(late, 1)
                        late = j
                    if between and between[0] == j:
                        between[1]()

            def top_layer1(c):
                pe.wait_ge(logits_split[c], 2)
                if c == 0:
                    pe.wait_ge(top_split, 2)
                for m in range(TILES1):
                    ms = slice(m * 128, (m + 1) * 128)
                    z = top_bank(1, c, m)
                    nc.tensor.matmul(z, wt1d_sb[:, ms], dense_sb[:, c * BANK:(c + 1) * BANK], start=True, stop=False)
                    for k in range(2):
                        hi_k, lo_k = logits_r[c][:, k, 0:BANK], logits_r[c][:, k, BANK:]
                        nc.tensor.matmul(z, wt1_hi[:, k, ms], hi_k, start=False, stop=False)
                        nc.tensor.matmul(z, wt1_lo[:, k, ms], hi_k, start=False, stop=False)
                        last = nc.tensor.matmul(z, wt1_hi[:, k, ms], lo_k, start=False, stop=k == 1)
                    last.then_inc(top1_done, 1)

            def top_layer2(c):
                for m in range(TILES2):
                    ms = slice(m * 128, (m + 1) * 128)
                    z = top_bank(2, c, m)
                    for k in range(TILES1):
                        if m == 0:
                            pe.wait_ge(top1_split[c], k + 1)
                        nc.tensor.matmul(z, wt2_hi[:, k, ms], top1_hi[c][:, k, :], start=k == 0, stop=False)
                        nc.tensor.matmul(z, wt2_lo[:, k, ms], top1_hi[c][:, k, :], start=False, stop=False)
                        last = nc.tensor.matmul(z, wt2_hi[:, k, ms], top1_lo[c][:, k, :], start=False,
                                                stop=k == TILES1 - 1)
                    last.then_inc(top2_done, 1)

            def top_layer3(c):
                pe.wait_ge(top1_rounded, TILES1 + c + 1)
                for k in range(TILES2):
                    pe.wait_ge(top2_ready, c * TILES2 + k + 1)
                    last = nc.tensor.matmul(top_bank(3, c, 0)[0:1, :], wt3_sb[:, k:k + 1],
                                            top2[:, k, c * BANK:(c + 1) * BANK],
                                            start=(k == 0), stop=(k == TILES2 - 1))
                last.then_inc(y_done, 1)

            pe.wait_ge(ident_ready, 1)
            transpose_rows(0, 0, xk[0])
            pe.wait_ge(wlo_ready, 1)
            contract(PROLOGUE, L0, L2, accumulator(0, 1))
            transpose_rows(1, 1, xk[1])
            pe.wait_ge(wlo_ready, 3)

            def step(n, parity):
                pe.wait_ge(z_evacuated[0], n + 1)
                contract(n, L1, L0, accumulator(1, parity))
                if not past_end(n, 1):
                    pe.wait_ge(z_evacuated[2], n + 1)
                    contract(n, L0, L2, accumulator(0, parity), None if past_end(n, 2) else
                             (L0 + 1, lambda: transpose_rows(n + 2, parity, xk[0])))
                if past_end(n, 1):
                    top_layer1(0)
                pe.wait_ge(z_evacuated[1], n + 1)
                contract(n, L2, STEP, accumulator(2, parity))

            each_step(pe, step)
            top_layer2(0)
            top_layer1(1)
            top_layer3(0)
            top_layer2(1)
            top_layer3(1)


def kernel(**inputs):
    import numpy as np
    import concourse.bacc as bacc
    from concourse import mybir as mb
    from concourse.bass_utils import run_bass_kernel_spmd

    def a(name):
        return np.asarray(inputs[name])

    field = (np.arange(2)[:, None] * PAIRS + np.arange(PAIRS)[None, :]) % FIELDS
    ids = a("ids").reshape(BLOCKS, BLOCK, FIELDS)[:, :, field]
    ids = ids.transpose(2, 1, 0, 3).reshape(128, BLOCKS * PAIRS)
    start = np.cumsum([0] + [a(f"tbl_{f}").shape[0] for f in range(FIELDS - 1)]).astype(np.int32)
    base = np.broadcast_to(start[field][:, None, None, :], (2, BLOCK, BLOCKS, PAIRS)).reshape(128, BLOCKS * PAIRS)

    row = np.arange(ROWS0)[:, None]
    h = row % FIELDS
    k = (h + PER * np.array(SPLITS[0] + FULLS[0])[None, :] + row // FIELDS) % FIELDS
    w0 = a("L0_rec_w0")

    def by_tile(w, l):
        def fields(t):
            return [first_field(t), first_field(t) + (t != SHORT)]

        return np.concatenate([w[fields(t)].reshape(128, LAYER) for t in SPLITS[l] + FULLS[l]])

    w1 = a("L0_rec_w1")
    b1 = a("L0_rec_b1")
    arrays = {
        "ids": ids,
        "base": base,
        "table": np.concatenate([a(f"tbl_{f}") for f in range(FIELDS)]),
        "w0": w0[h, k],
        "w0t": w0[k, h],
        "w1": by_tile(np.concatenate([w1[:, :, NEXT:], w1[:, :, :NEXT]], axis=2), 1),
        "w2": by_tile(a("L0_rec_w2"), 2),
        "b0": a("L0_rec_b0").reshape(LAYER, 1),
        "b1": np.concatenate([b1[NEXT:], b1[:NEXT]]).reshape(LAYER, 1),
        "b2": a("L0_rec_b2").reshape(LAYER, 1),
        "dense": a("dense_ctx").T,
        "wt1": a("W_top1"),
        "bt1": a("b_top1").reshape(TOP1 // 128, 128).T,
        "wt2": a("W_top2"),
        "bt2": a("b_top2").reshape(TOP2 // 128, 128).T,
        "wt3": a("W_top3").reshape(TOP2 // 128, 128).T,
    }
    arrays = {n: np.ascontiguousarray(v) for n, v in arrays.items()}

    nc = bacc.Bacc("TRN2", target_bir_lowering=False, num_devices=1, dynamic_dma_scratch_size=4096)
    aps = [nc.dram_tensor(n, v.shape, mb.dt.from_np(v.dtype), kind="ExternalInput").ap() for n, v in arrays.items()]
    out = nc.dram_tensor("out", (BATCH, 1), mb.dt.float32, kind="ExternalOutput").ap()
    build(nc, *aps, out)
    r = run_bass_kernel_spmd(nc, [arrays], core_ids=[0])
    return r.results[0]["out"]
```
